# Optimizing a Trainium2 kernel written in Bass

```python
import numpy as np
import jax
import jax.numpy as jnp

def _softmax(x, axis=-1):
    return jax.nn.softmax(x, axis=axis)

def _gelu(x):
    return jax.nn.gelu(x, approximate=True)

def _silu(x):
    return jax.nn.silu(x)

def _sigmoid(x):
    return jax.nn.sigmoid(x)

def _layernorm(x, axis=-1, eps=1e-05):
    m = jnp.mean(x, axis=axis, keepdims=True)
    v = jnp.var(x, axis=axis, keepdims=True)
    return (x - m) / jnp.sqrt(v + eps)

def _scatter_add(tgt, idx, src, axis=0):
    return tgt.at[idx].add(src)

def _segment_sum(src, seg, n):
    return jax.ops.segment_sum(src, seg, n)
kernel_name = 'mk_dlrm_tower_d1_rec_r8_e3bb91'

def setup_inputs(seed: int=0):
    np.random.seed(seed)
    _w = jnp.asarray

    def _rec_inputs():
        import jax
        import jax.numpy as jnp
        _tk = jax.random.key(seed)
        ids = jnp.stack([jax.random.randint(jax.random.fold_in(_tk, 200 + f), (2048,), 0, v, jnp.int32) for f, v in enumerate([125000, 12500, 12500, 1000, 1000, 12500, 1250, 12500, 12500, 1000, 1250, 12500, 12500, 1000, 1000, 12500, 1250, 1000, 1250, 12500, 1000, 1000, 1000, 1000, 1000, 1000])], axis=1)
        tbl_0 = 0.05 * jax.random.normal(jax.random.fold_in(_tk, 500 + 0), (125000, 128), jnp.float32)
        tbl_1 = 0.05 * jax.random.normal(jax.random.fold_in(_tk, 500 + 1), (12500, 128), jnp.float32)
        tbl_2 = 0.05 * jax.random.normal(jax.random.fold_in(_tk, 500 + 2), (12500, 128), jnp.float32)
        tbl_3 = 0.05 * jax.random.normal(jax.random.fold_in(_tk, 500 + 3), (1000, 128), jnp.float32)
        tbl_4 = 0.05 * jax.random.normal(jax.random.fold_in(_tk, 500 + 4), (1000, 128), jnp.float32)
        tbl_5 = 0.05 * jax.random.normal(jax.random.fold_in(_tk, 500 + 5), (12500, 128), jnp.float32)
        tbl_6 = 0.05 * jax.random.normal(jax.random.fold_in(_tk, 500 + 6), (1250, 128), jnp.float32)
        tbl_7 = 0.05 * jax.random.normal(jax.random.fold_in(_tk, 500 + 7), (12500, 128), jnp.float32)
        tbl_8 = 0.05 * jax.random.normal(jax.random.fold_in(_tk, 500 + 8), (12500, 128), jnp.float32)
        tbl_9 = 0.05 * jax.random.normal(jax.random.fold_in(_tk, 500 + 9), (1000, 128), jnp.float32)
        tbl_10 = 0.05 * jax.random.normal(jax.random.fold_in(_tk, 500 + 10), (1250, 128), jnp.float32)
        tbl_11 = 0.05 * jax.random.normal(jax.random.fold_in(_tk, 500 + 11), (12500, 128), jnp.float32)
        tbl_12 = 0.05 * jax.random.normal(jax.random.fold_in(_tk, 500 + 12), (12500, 128), jnp.float32)
        tbl_13 = 0.05 * jax.random.normal(jax.random.fold_in(_tk, 500 + 13), (1000, 128), jnp.float32)
        tbl_14 = 0.05 * jax.random.normal(jax.random.fold_in(_tk, 500 + 14), (1000, 128), jnp.float32)
        tbl_15 = 0.05 * jax.random.normal(jax.random.fold_in(_tk, 500 + 15), (12500, 128), jnp.float32)
        tbl_16 = 0.05 * jax.random.normal(jax.random.fold_in(_tk, 500 + 16), (1250, 128), jnp.float32)
        tbl_17 = 0.05 * jax.random.normal(jax.random.fold_in(_tk, 500 + 17), (1000, 128), jnp.float32)
        tbl_18 = 0.05 * jax.random.normal(jax.random.fold_in(_tk, 500 + 18), (1250, 128), jnp.float32)
        tbl_19 = 0.05 * jax.random.normal(jax.random.fold_in(_tk, 500 + 19), (12500, 128), jnp.float32)
        tbl_20 = 0.05 * jax.random.normal(jax.random.fold_in(_tk, 500 + 20), (1000, 128), jnp.float32)
        tbl_21 = 0.05 * jax.random.normal(jax.random.fold_in(_tk, 500 + 21), (1000, 128), jnp.float32)
        tbl_22 = 0.05 * jax.random.normal(jax.random.fold_in(_tk, 500 + 22), (1000, 128), jnp.float32)
        tbl_23 = 0.05 * jax.random.normal(jax.random.fold_in(_tk, 500 + 23), (1000, 128), jnp.float32)
        tbl_24 = 0.05 * jax.random.normal(jax.random.fold_in(_tk, 500 + 24), (1000, 128), jnp.float32)
        tbl_25 = 0.05 * jax.random.normal(jax.random.fold_in(_tk, 500 + 25), (1000, 128), jnp.float32)
        _rk = jax.random.fold_in(_tk, 7)
        r_bottom_output = -0.000520686 + 1.00062 * jax.random.normal(jax.random.fold_in(_rk, 101), (2048, 128), jnp.float32)
        W_top1 = 0.0456912 * jax.random.normal(jax.random.fold_in(_tk, 801), (479, 512), jnp.float32)
        W_top2 = 0.0441942 * jax.random.normal(jax.random.fold_in(_tk, 802), (512, 256), jnp.float32)
        W_top3 = 0.0625 * jax.random.normal(jax.random.fold_in(_tk, 803), (256, 1), jnp.float32)
        b_top1 = jnp.zeros((512,), jnp.float32)
        b_top2 = jnp.zeros((256,), jnp.float32)
        return (r_bottom_output, ids, tbl_0, tbl_1, tbl_2, tbl_3, tbl_4, tbl_5, tbl_6, tbl_7, tbl_8, tbl_9, tbl_10, tbl_11, tbl_12, tbl_13, tbl_14, tbl_15, tbl_16, tbl_17, tbl_18, tbl_19, tbl_20, tbl_21, tbl_22, tbl_23, tbl_24, tbl_25, W_top1, b_top1, W_top2, b_top2, W_top3)
    r_bottom_output, ids, tbl_0, tbl_1, tbl_2, tbl_3, tbl_4, tbl_5, tbl_6, tbl_7, tbl_8, tbl_9, tbl_10, tbl_11, tbl_12, tbl_13, tbl_14, tbl_15, tbl_16, tbl_17, tbl_18, tbl_19, tbl_20, tbl_21, tbl_22, tbl_23, tbl_24, tbl_25, W_top1, b_top1, W_top2, b_top2, W_top3 = _rec_inputs()

    def _L0_rec_setup():
        import jax, jax.numpy as jnp
        import numpy as np
        NUM_FEATURES = 27
        _TRIU_I, _TRIU_J = np.triu_indices(NUM_FEATURES, k=1)
        key = jax.random.key(seed)
        k1, k2 = jax.random.split(key)
        bottom_output = jax.random.normal(k1, (2048, 128), dtype=jnp.float32)
        embeddings = jax.random.normal(k2, (2048, 26, 128), dtype=jnp.float32)
        return {'bottom_output': bottom_output, 'embeddings': embeddings}
    _L0_rec_all = _L0_rec_setup()
    _L0_rec_in = {k: v for k, v in _L0_rec_all.items() if k in ()}
    del _L0_rec_all
    return {'r_bottom_output': r_bottom_output, 'ids': ids, 'tbl_0': tbl_0, 'tbl_1': tbl_1, 'tbl_2': tbl_2, 'tbl_3': tbl_3, 'tbl_4': tbl_4, 'tbl_5': tbl_5, 'tbl_6': tbl_6, 'tbl_7': tbl_7, 'tbl_8': tbl_8, 'tbl_9': tbl_9, 'tbl_10': tbl_10, 'tbl_11': tbl_11, 'tbl_12': tbl_12, 'tbl_13': tbl_13, 'tbl_14': tbl_14, 'tbl_15': tbl_15, 'tbl_16': tbl_16, 'tbl_17': tbl_17, 'tbl_18': tbl_18, 'tbl_19': tbl_19, 'tbl_20': tbl_20, 'tbl_21': tbl_21, 'tbl_22': tbl_22, 'tbl_23': tbl_23, 'tbl_24': tbl_24, 'tbl_25': tbl_25, 'W_top1': W_top1, 'b_top1': b_top1, 'W_top2': W_top2, 'b_top2': b_top2, 'W_top3': W_top3}

def reference(r_bottom_output, ids, tbl_0, tbl_1, tbl_2, tbl_3, tbl_4, tbl_5, tbl_6, tbl_7, tbl_8, tbl_9, tbl_10, tbl_11, tbl_12, tbl_13, tbl_14, tbl_15, tbl_16, tbl_17, tbl_18, tbl_19, tbl_20, tbl_21, tbl_22, tbl_23, tbl_24, tbl_25, W_top1, b_top1, W_top2, b_top2, W_top3):
    import jax
    import jax.numpy as jnp

    def _L0_rec_ref(bottom_output, embeddings):
        import jax, jax.numpy as jnp
        import numpy as np
        NUM_FEATURES = 27
        _TRIU_I, _TRIU_J = np.triu_indices(NUM_FEATURES, k=1)
        all_emb = jnp.concatenate([bottom_output[:, None, :], embeddings], axis=1)
        gram = jnp.einsum('bfd,bgd->bfg', all_emb, all_emb)
        return gram[:, _TRIU_I, _TRIU_J]
    e = jnp.stack([tbl_0[ids[:, 0]], tbl_1[ids[:, 1]], tbl_2[ids[:, 2]], tbl_3[ids[:, 3]], tbl_4[ids[:, 4]], tbl_5[ids[:, 5]], tbl_6[ids[:, 6]], tbl_7[ids[:, 7]], tbl_8[ids[:, 8]], tbl_9[ids[:, 9]], tbl_10[ids[:, 10]], tbl_11[ids[:, 11]], tbl_12[ids[:, 12]], tbl_13[ids[:, 13]], tbl_14[ids[:, 14]], tbl_15[ids[:, 15]], tbl_16[ids[:, 16]], tbl_17[ids[:, 17]], tbl_18[ids[:, 18]], tbl_19[ids[:, 19]], tbl_20[ids[:, 20]], tbl_21[ids[:, 21]], tbl_22[ids[:, 22]], tbl_23[ids[:, 23]], tbl_24[ids[:, 24]], tbl_25[ids[:, 25]]], axis=1)
    z = _L0_rec_ref(r_bottom_output, e)
    z = z.reshape(z.shape[0], -1)
    h = jnp.concatenate([z, r_bottom_output], axis=1)
    h = jnp.maximum(h @ W_top1 + b_top1, 0.0)
    h = jnp.maximum(h @ W_top2 + b_top2, 0.0)
    y = h @ W_top3
    return y

_drawn_inputs = setup_inputs


def setup_inputs(seed=0):
    import zlib

    import numpy as np

    out = dict(_drawn_inputs(seed))
    spreads = {'b_top1': (0.0, 0.1), 'b_top2': (0.0, 0.1)}
    factors = {}
    for name, (base, spread) in spreads.items():
        noise = np.random.default_rng([zlib.crc32(name.encode()), seed]).standard_normal(out[name].shape)
        drawn = base * np.exp(spread * noise) if base else spread * noise
        out[name] = jnp.asarray(drawn.astype(out[name].dtype))
    for name, factor in factors.items():
        out[name] = (out[name] * factor).astype(out[name].dtype)
    return out
```

```python
from contextlib import ExitStack

import concourse.bass as bass
from concourse import mybir

P = 128
D = 128
BATCH = 2048
TABLES = 26
SLOTS = TABLES + 1
BLOCK_TILES = 4
BLOCKS = BATCH // (P * BLOCK_TILES)
TILES = BLOCKS * BLOCK_TILES
BLOCK = P * BLOCK_TILES
HIDDEN1, HIDDEN2 = 512, 256
M1, M2 = HIDDEN1 // P, HIDDEN2 // P

GROUP = 4
GROUPS = -(-TABLES // GROUP)
RING = 2
SIZES = [min(GROUP, TABLES - GROUP * g) for g in range(GROUPS)]

QUADRANT = 32
COLUMNS = [7, 7, 6, 6]
COLUMNS_FROM = [1, 8, 15, 21]
PAIR_TILES = max(COLUMNS)
K1 = PAIR_TILES + 1

F32 = mybir.dt.float32
F32R = mybir.dt.float32r
I32 = mybir.dt.int32
ALU = mybir.AluOpType
ACT = mybir.ActivationFunctionType


def dlrm_tower(nc, xT, ids, tables, w1, b1, w2, b2, w3, out):
    with ExitStack() as ctx:
        def sb(name, shape, dt=F32):
            return ctx.enter_context(nc.sbuf_tensor(name, shape, dt))

        def psum(name, shape):
            return ctx.enter_context(nc.psum_tensor(name, shape, F32))

        def sem(name):
            return ctx.enter_context(nc.semaphore(name))

        identity = sb("identity", [P, P])
        index = [sb(f"index{h}", [P, 2 * TABLES], I32) for h in range(2)]
        rows = sb("rows", [P, RING, TABLES, D])
        features = sb("features", [P, BLOCK_TILES, P, SLOTS])
        bottom = sb("bottom", [P, BATCH])
        bottom_hi = sb("bottom_hi", [P, BLOCK], F32R)
        bottom_lo = sb("bottom_lo", [P, BLOCK], F32R)
        pairs = sb("pairs", [P, 2, PAIR_TILES, P])
        pairs_hi = sb("pairs_hi", [P, PAIR_TILES, BLOCK], F32R)
        pairs_lo = sb("pairs_lo", [P, PAIR_TILES, BLOCK], F32R)
        w1_hi = sb("w1_hi", [P, K1, HIDDEN1], F32R)
        w1_lo = sb("w1_lo", [P, K1, HIDDEN1], F32R)
        w2_hi = sb("w2_hi", [P, M1, HIDDEN2], F32R)
        w2_lo = sb("w2_lo", [P, M1, HIDDEN2], F32R)
        b1_sb = sb("b1_sb", [P, M1])
        b2_sb = sb("b2_sb", [P, M2])
        w3_sb = sb("w3_sb", [P, M2])
        h1 = sb("h1", [P, 2, BLOCK])
        h1_hi = sb("h1_hi", [P, M1, BLOCK], F32R)
        h1_lo = sb("h1_lo", [P, M1, BLOCK], F32R)
        h2 = sb("h2", [P, M2, BLOCK])
        y_sb = sb("y_sb", [P, TILES])

        late = features[:, 2:4].rearrange("p q b s -> p (q b s)")
        w1_raw = late[:, 0:K1 * HIDDEN1].rearrange("p (k n) -> p k n", k=K1)
        w2_raw = late[:, K1 * HIDDEN1:K1 * HIDDEN1 + M1 * HIDDEN2].rearrange("p (k n) -> p k n", k=M1)

        turned = psum("turned", [P, 2, GROUP, P])
        gram = psum("gram", [P, 2, P // 4, QUADRANT])
        acc = psum("acc", [P, 2, BLOCK])

        index_landed = [sem(f"index_landed{h}") for h in range(2)]
        rows_landed = [[sem(f"rows_landed{r}_{g}") for g in range(GROUPS)] for r in range(RING)]
        bottom_landed = sem("bottom_landed")
        w1_landed = sem("w1_landed")
        w2_landed = sem("w2_landed")
        small_landed = sem("small_landed")
        identity_zero = sem("identity_zero")
        identity_ready = sem("identity_ready")
        pairs_cleared = sem("pairs_cleared")
        weights_split = sem("weights_split")
        transposed = sem("transposed")
        grammed = sem("grammed")
        accumulated = sem("accumulated")
        turned_out = sem("turned_out")
        act_regrouped = sem("act_regrouped")
        acc_out = sem("acc_out")
        dve_regrouped = sem("dve_regrouped")
        slot0_ready = sem("slot0_ready")
        bottom_split = sem("bottom_split")
        pairs_high = sem("pairs_high")
        pairs_split = sem("pairs_split")
        h1_high = sem("h1_high")
        h1_split = sem("h1_split")
        out_landed = sem("out_landed")

        PRIME_TURNED = 2
        PRIME_ROWS = RING * GROUPS
        PRIME_TILES = 4
        FILLS = M1 + M2 + 1

        gate = {name: sem(f"gate_{name}") for name in ("sp", "pool", "dve")}

        def gated(eng, name, sem, count):
            eng.wait_ge(sem, count)
            eng.sem_inc(gate[name], 1)

        block = ctx.enter_context(nc.Block())

        @block.sync
        def _(sp):
            for h in range(2):
                sp.dma_start(index[h][:], ids[0, h]).then_inc(index_landed[h], 16)
            sp.dma_start(bottom[:], xT).then_inc(bottom_landed, 16)
            sp.dma_start(w1_raw, w1).then_inc(w1_landed, 16)
            sp.dma_start(w2_raw, w2).then_inc(w2_landed, 16)
            for to, of in ((b1_sb, b1), (b2_sb, b2), (w3_sb, w3)):
                sp.dma_start(to[:], of).then_inc(small_landed, 16)
            with sp.Fori(0, BLOCKS - 1) as b:
                for h in range(2):
                    for r in range(RING):
                        for g in range(GROUPS):
                            gated(sp, "sp", rows_landed[r][g], b * (2 * 16 * SIZES[g]) + 16 * SIZES[g] * (h + 1))
                    sp.dma_start(index[h][:], ids[bass.ds(b + 1, 1), h].rearrange("o p i -> (o p) i")).then_inc(
                        index_landed[h], 16)
            sp.wait_ge(acc_out, 1 + FILLS * BLOCKS)
            sp.dma_start(out, y_sb[:]).then_inc(out_landed, 16)
            sp.wait_ge(out_landed, 16)

        @block.gpsimd
        def _(pool):
            pool.memset(identity[:], 0.0).then_inc(identity_zero, 1)
            pool.wait_ge(identity_zero, 1)
            pool.affine_select(out=identity[:], in_=identity[:], compare_op=ALU.not_equal, fill=1.0,
                               base=0, pattern=[[-1, P]], channel_multiplier=1).then_inc(identity_ready, 1)
            with pool.Fori(0, BLOCKS) as b:
                for q in range(BLOCK_TILES):
                    if q % 2 == 0:
                        pool.wait_ge(index_landed[q // 2], b * 16 + 16)
                    for g in range(GROUPS):
                        gated(pool, "pool", transposed, b * (BLOCK_TILES * GROUPS) + q * GROUPS + g + 1)
                        for f in range(GROUP * g, GROUP * g + SIZES[g]):
                            at = (q % 2) * TABLES + f
                            pool.indirect_dma_start(
                                out=rows[:, q % RING, f, :], out_offset=None, in_=tables[f],
                                in_offset=bass.IndirectOffsetOnAxis(ap=index[q // 2][:, at:at + 1], axis=0),
                            ).then_inc(rows_landed[q % RING][g], 16)

        @block.tensor
        def _(pe):
            pe.sem_inc(transposed, PRIME_ROWS)
            pe.sem_inc(grammed, PRIME_TILES)

            def transpose_tile(b, q):
                for g in range(GROUPS):
                    n = q * GROUPS + g
                    pe.wait_ge(rows_landed[q % RING][g], b * (2 * 16 * SIZES[g]) + 16 * SIZES[g] * (q // 2 + 1))
                    pe.wait_ge(turned_out, b * (BLOCK_TILES * GROUPS) + n + 1)
                    for i in range(SIZES[g]):
                        last = pe.transpose(turned[:, n % 2, i, :], rows[:, q % RING, GROUP * g + i, :], identity[:])
                    last.then_inc(transposed, 1)

            def gram_tile(b, q):
                pe.wait_ge(turned_out, b * (BLOCK_TILES * GROUPS) + (q + 1) * GROUPS + PRIME_TURNED)
                pe.wait_ge(slot0_ready, b * BLOCK_TILES + q + 1)
                pe.wait_ge(act_regrouped, b * BLOCK_TILES + q + 1)
                pe.wait_ge(dve_regrouped, b * BLOCK_TILES + q + 1)
                for i in range(P):
                    s = i % 4
                    last = pe.matmul(gram[QUADRANT * s:QUADRANT * s + SLOTS, q % 2, i // 4, 0:SLOTS - 1],
                                     features[:, q, i, :], features[:, q, i, 1:SLOTS], start=True, stop=True)
                last.then_inc(grammed, 1)

            def product(to, w_hi, w_lo, x_hi, x_lo, first, last):
                pe.matmul(to, w_hi, x_hi, start=first, stop=False)
                pe.matmul(to, w_hi, x_lo, start=False, stop=False)
                return pe.matmul(to, w_lo, x_hi, start=False, stop=last)

            pe.wait_ge(identity_ready, 1)
            with pe.Fori(0, BLOCKS) as b:
                transpose_tile(b, 0)
                for q in range(BLOCK_TILES):
                    if q + 1 < BLOCK_TILES:
                        transpose_tile(b, q + 1)
                    gram_tile(b, q)

                pe.wait_ge(weights_split, 4)
                pe.wait_ge(bottom_split, b * 2 + 2)
                for m in range(M1):
                    if m != 1:
                        pe.wait_ge(acc_out, b * FILLS + max(m - 1, 0) + 1)
                    at = slice(m * P, (m + 1) * P)
                    for k in (PAIR_TILES, *range(PAIR_TILES)):
                        if k == 0 and m == 0:
                            pe.wait_ge(pairs_split, b * BLOCK_TILES + BLOCK_TILES + 2)
                        x_hi, x_lo = ((bottom_hi[:], bottom_lo[:]) if k == PAIR_TILES
                                      else (pairs_hi[:, k, :], pairs_lo[:, k, :]))
                        last = product(acc[:, m % 2, :], w1_hi[:, k, at], w1_lo[:, k, at], x_hi, x_lo,
                                       k == PAIR_TILES, k == PAIR_TILES - 1)
                    last.then_inc(accumulated, 1)

                for m in range(M2):
                    pe.wait_ge(acc_out, b * FILLS + M1 - 1 + m + 1)
                    at = slice(m * P, (m + 1) * P)
                    for k in range(M1):
                        if m == 0:
                            pe.wait_ge(h1_split, b * M1 + k + 1 + 2)
                        last = product(acc[:, m, :], w2_hi[:, k, at], w2_lo[:, k, at], h1_hi[:, k, :], h1_lo[:, k, :],
                                       k == 0, k == M1 - 1)
                    last.then_inc(accumulated, 1)

                pe.wait_ge(acc_out, b * FILLS + M1 + M2 + 1)
                for q in range(BLOCK_TILES):
                    for k in range(M2):
                        last = pe.matmul(acc[:, 0, q:q + 1], h2[:, k, q * P:(q + 1) * P], w3_sb[:, k:k + 1],
                                         start=(k == 0), stop=(k == M2 - 1))
                last.then_inc(accumulated, 1)

        def regroup(eng, copy, q, quadrants):
            for s in quadrants:
                for j in range(4):
                    at = COLUMNS_FROM[j] - 1
                    last = copy(
                        pairs[QUADRANT * j:QUADRANT * j + SLOTS, q % 2, 0:COLUMNS[j], :].rearrange(
                            "f k (t s) -> f s k t", s=4)[:, s],
                        gram[QUADRANT * s:QUADRANT * s + SLOTS, q % 2, :, at:at + COLUMNS[j]].rearrange(
                            "f t k -> f k t"))
            return last

        @block.scalar
        def _(act):
            act.sem_inc(turned_out, PRIME_TURNED)
            act.sem_inc(act_regrouped, 2)
            act.sem_inc(acc_out, 1)

            def turned_tile(b, q):
                act.wait_ge(grammed, b * BLOCK_TILES + q + 1)
                if q == 2:
                    act.wait_ge(weights_split, 4)
                for g in range(GROUPS):
                    n = q * GROUPS + g
                    act.wait_ge(transposed, b * (BLOCK_TILES * GROUPS) + n + 1 + PRIME_ROWS)
                    at = 1 + GROUP * g
                    nc.scalar.copy(features[:, q, :, at:at + SIZES[g]].rearrange("d b f -> d f b"),
                                   turned[:, n % 2, 0:SIZES[g], :]).then_inc(turned_out, 1)

            def regroup_tile(b, q):
                act.wait_ge(grammed, b * BLOCK_TILES + q + 1 + PRIME_TILES)
                act.wait_ge(pairs_split, b * BLOCK_TILES + q + 1)
                regroup(act, nc.scalar.copy, q, (0, 1)).then_inc(act_regrouped, 1)

            act.wait_ge(small_landed, 3 * 16)
            act.wait_ge(pairs_cleared, 1)
            with act.Fori(0, BLOCKS) as b:
                turned_tile(b, 0)
                turned_tile(b, 1)
                turned_tile(b, 2)
                regroup_tile(b, 0)
                turned_tile(b, 3)
                for q in range(1, BLOCK_TILES):
                    regroup_tile(b, q)
                for m in range(M1):
                    act.wait_ge(accumulated, b * FILLS + m + 1)
                    act.wait_ge(h1_split, b * M1 + m + 1)
                    nc.scalar.activation(h1[:, m % 2, :], acc[:, m % 2, :], ACT.Relu,
                                         bias=b1_sb[:, m:m + 1]).then_inc(acc_out, 1)
                for m in range(M2):
                    act.wait_ge(accumulated, b * FILLS + M1 + m + 1)
                    nc.scalar.activation(h2[:, m, :], acc[:, m, :], ACT.Relu,
                                         bias=b2_sb[:, m:m + 1]).then_inc(acc_out, 1)
                act.wait_ge(accumulated, b * FILLS + FILLS)
                nc.scalar.copy(y_sb[:, bass.ds(b * BLOCK_TILES, BLOCK_TILES)],
                               acc[:, 0, 0:BLOCK_TILES]).then_inc(acc_out, 1)

        @block.vector
        def _(dve):
            dve.sem_inc(dve_regrouped, 2)
            dve.sem_inc(pairs_split, 2)
            dve.sem_inc(h1_split, 2)

            dve.memset(pairs[:], 0.0).then_inc(pairs_cleared, 1)
            dve.wait_ge(w1_landed, 16)
            dve.tensor_copy(w1_hi[:], w1_raw).then_inc(weights_split, 1)
            dve.wait_ge(w2_landed, 16)
            dve.tensor_copy(w2_hi[:], w2_raw).then_inc(weights_split, 1)
            dve.wait_ge(weights_split, 2)
            dve.tensor_tensor(w1_lo[:], w1_raw, w1_hi[:], ALU.subtract).then_inc(weights_split, 1)
            dve.tensor_tensor(w2_lo[:], w2_raw, w2_hi[:], ALU.subtract).then_inc(weights_split, 1)
            dve.wait_ge(weights_split, 4)
            dve.wait_ge(bottom_landed, 16)
            dve.wait_ge(pairs_cleared, 1)

            def split_tile(b, q):
                if q == 0:
                    pass
                dve.wait_ge(act_regrouped, b * BLOCK_TILES + q + 1 + 2)
                dve.wait_ge(dve_regrouped, b * BLOCK_TILES + q + 1 + 2)
                at = slice(q * P, (q + 1) * P)
                dve.tensor_copy(pairs_hi[:, :, at], pairs[:, q % 2]).then_inc(pairs_high, 1)
                dve.wait_ge(pairs_high, b * BLOCK_TILES + q + 1)
                dve.tensor_tensor(pairs_lo[:, :, at], pairs[:, q % 2], pairs_hi[:, :, at],
                                  ALU.subtract).then_inc(pairs_split, 1)

            with dve.Fori(0, BLOCKS) as b:
                for q in range(BLOCK_TILES):
                    gated(dve, "dve", grammed, b * BLOCK_TILES + q + 1)
                    dve.tensor_copy(features[:, q, :, 0],
                                    bottom[:, bass.ds(b * BLOCK + q * P, P)]).then_inc(slot0_ready, 1)
                gated(dve, "dve", acc_out, b * FILLS + 1)
                dve.tensor_copy(bottom_hi[:], bottom[:, bass.ds(b * BLOCK, BLOCK)]).then_inc(bottom_split, 1)
                gated(dve, "dve", bottom_split, b * 2 + 1)
                dve.tensor_tensor(bottom_lo[:], bottom[:, bass.ds(b * BLOCK, BLOCK)], bottom_hi[:],
                                  ALU.subtract).then_inc(bottom_split, 1)
                for q in range(BLOCK_TILES):
                    dve.wait_ge(grammed, b * BLOCK_TILES + q + 1 + PRIME_TILES)
                    dve.wait_ge(pairs_split, b * BLOCK_TILES + q + 1)
                    regroup(dve, dve.tensor_copy, q, (2, 3)).then_inc(dve_regrouped, 1)
                    split_tile(b, q)
                for m in range(M1):
                    dve.wait_ge(acc_out, b * FILLS + m + 1 + 1)
                    dve.tensor_copy(h1_hi[:, m, :], h1[:, m % 2, :]).then_inc(h1_high, 1)
                    dve.wait_ge(h1_high, b * M1 + m + 1)
                    dve.tensor_tensor(h1_lo[:, m, :], h1[:, m % 2, :], h1_hi[:, m, :],
                                      ALU.subtract).then_inc(h1_split, 1)


def layer1_rows():
    import numpy as np

    number = {}
    for f in range(SLOTS):
        for g in range(f + 1, SLOTS):
            number[f, g] = len(number)
    at = np.full((P, PAIR_TILES), -1)
    for j in range(4):
        for k in range(COLUMNS[j]):
            g = COLUMNS_FROM[j] + k
            for f in range(g):
                at[QUADRANT * j + f, k] = number[f, g]
    return at, len(number)


def kernel(**inputs):
    import numpy as np
    import concourse.bacc as bacc
    from concourse.bass_utils import run_bass_kernel_spmd

    a = {name: np.asarray(v) for name, v in inputs.items()}
    at, pairs = layer1_rows()
    w1 = np.zeros((P, K1, HIDDEN1), np.float32)
    w1[:, :PAIR_TILES][at >= 0] = a["W_top1"][at[at >= 0]]
    w1[:, PAIR_TILES] = a["W_top1"][pairs:]
    arrays = {
        "in_xT": a["r_bottom_output"].reshape(P, TILES, D).transpose(2, 1, 0).reshape(D, BATCH),
        "in_ids": a["ids"].reshape(P, BLOCKS, 2, 2 * TABLES).transpose(1, 2, 0, 3),
        "in_w1": w1,
        "in_b1": a["b_top1"].reshape(M1, P).T,
        "in_w2": a["W_top2"].reshape(M1, P, HIDDEN2).transpose(1, 0, 2),
        "in_b2": a["b_top2"].reshape(M2, P).T,
        "in_w3": a["W_top3"].reshape(M2, P).T,
    }
    for f in range(TABLES):
        arrays[f"in_tbl_{f}"] = a[f"tbl_{f}"]
    arrays = {name: np.ascontiguousarray(x) for name, x in arrays.items()}

    nc = bacc.Bacc("TRN2", target_bir_lowering=False, num_devices=1)
    ap = {name: nc.dram_tensor(name, x.shape, mybir.dt.from_np(x.dtype), kind="ExternalInput").ap()
          for name, x in arrays.items()}
    out = nc.dram_tensor("out", (BATCH, 1), F32, kind="ExternalOutput").ap()
    dlrm_tower(nc, ap["in_xT"], ap["in_ids"], [ap[f"in_tbl_{f}"] for f in range(TABLES)],
               ap["in_w1"], ap["in_b1"], ap["in_w2"], ap["in_b2"], ap["in_w3"],
               out.rearrange("(p t) o -> p (t o)", p=P))
    r = run_bass_kernel_spmd(nc, [arrays], core_ids=[0])
    return r.results[0]["out"]
```

```python
from contextlib import ExitStack

import concourse.bass as bass
from concourse import mybir

P = 128
D = 128
BATCH = 2048
TABLES = 26
SLOTS = TABLES + 1
BLOCK_TILES = 4
BLOCKS = BATCH // (P * BLOCK_TILES)
TILES = BLOCKS * BLOCK_TILES
BLOCK = P * BLOCK_TILES
HIDDEN1, HIDDEN2 = 512, 256
M1, M2 = HIDDEN1 // P, HIDDEN2 // P

ONEHOT = [3, 4, 9, 13, 14, 17, 20]
ONEHOT_ROWS = 1000
CHUNKS = 8
ROW_PARTS = ONEHOT_ROWS // CHUNKS
NH = len(ONEHOT)
GATHERED = [f for f in range(TABLES) if f not in ONEHOT]
NG = len(GATHERED)
SLOT_TABLES = GATHERED + ONEHOT

GROUP = 4
GROUPS = -(-NG // GROUP)
SIZES = [min(GROUP, NG - GROUP * g) for g in range(GROUPS)]
BLOCK_GROUPS = BLOCK_TILES * GROUPS
RING = 2

QUADRANT = 32
GRAM = SLOTS - 1
TABLE_RING = 3

COLUMNS_FROM = [15, 19, 23, 11]
PAIR_TILES = 4
COLUMN_ROWS = [c + PAIR_TILES - 1 for c in COLUMNS_FROM]
ASIDE = 10
ASIDE_MOVES = [(7, 4, 10), (3, 4, 6), (1, 2, 2)]
FREE_ROW = QUADRANT * 3 + COLUMN_ROWS[3]
assert FREE_ROW + sum(n for _, _, n in ASIDE_MOVES) == P
K1 = PAIR_TILES + 1

F32 = mybir.dt.float32
F32R = mybir.dt.float32r
I32 = mybir.dt.int32
ALU = mybir.AluOpType
ACT = mybir.ActivationFunctionType


def dlrm_tower(nc, xT, ids, onehot_ids, row_numbers, gathered, onehot_tables, w1, b1, w2, b2, w3, out):
    with ExitStack() as ctx:
        def sb(name, shape, dt=F32):
            return ctx.enter_context(nc.sbuf_tensor(name, shape, dt))

        def psum(name, shape):
            return ctx.enter_context(nc.psum_tensor(name, shape, F32))

        def sem(name):
            return ctx.enter_context(nc.semaphore(name))

        identity = sb("identity", [P, P])
        index = [sb(f"index{h}", [P, 2 * NG], I32) for h in range(2)]
        rows = sb("rows", [P, RING, NG, D])
        features = sb("features", [P, BLOCK_TILES, P, SLOTS])
        bottom = sb("bottom", [P, BATCH])
        bottom_hi = sb("bottom_hi", [P, BLOCK], F32R)
        bottom_lo = sb("bottom_lo", [P, BLOCK], F32R)
        row_number = sb("row_number", [P, CHUNKS])
        table_raw = sb("table_raw", [P, 2, CHUNKS, D])
        table_hi = sb("table_hi", [P, TABLE_RING, CHUNKS, D], F32R)
        table_lo = sb("table_lo", [P, TABLE_RING, CHUNKS, D], F32R)
        wanted = sb("wanted", [P, 2, BLOCK], I32)
        pairs = sb("pairs", [P, 2, PAIR_TILES, P])
        aside = sb("aside", [P, 2, ASIDE, P])
        pairs_hi = sb("pairs_hi", [P, PAIR_TILES, BLOCK], F32R)
        pairs_lo = sb("pairs_lo", [P, PAIR_TILES, BLOCK], F32R)
        w1_hi = sb("w1_hi", [P, K1, HIDDEN1], F32R)
        w1_lo = sb("w1_lo", [P, K1, HIDDEN1], F32R)
        w2_hi = sb("w2_hi", [P, M1, HIDDEN2], F32R)
        w2_lo = sb("w2_lo", [P, M1, HIDDEN2], F32R)
        b1_sb = sb("b1_sb", [P, M1])
        b2_sb = sb("b2_sb", [P, M2])
        w3_sb = sb("w3_sb", [P, M2])
        h1 = sb("h1", [P, 2, BLOCK])
        h2 = sb("h2", [P, M2, BLOCK])
        y_sb = sb("y_sb", [1, BLOCK])
        onehot = sb("onehot", [P, CHUNKS, BLOCK], F32R)
        h1_hi = onehot[:, 0:M1]
        h1_lo = onehot[:, M1:2 * M1]
        w1_raw = aside[:].rearrange("p r c n -> p (r c n)").rearrange("p (k n) -> p k n", k=K1)
        w2_raw = h1[:].rearrange("p r n -> p (r n)").rearrange("p (k n) -> p k n", k=M1)

        turned = psum("turned", [P, 2, GROUP, P])
        gram = psum("gram", [P, 2, P // 4, QUADRANT])
        acc = psum("acc", [P, 2, BLOCK])

        index_landed = [sem(f"index_landed{h}") for h in range(2)]
        rows_landed = [[sem(f"rows_landed{r}_{g}") for g in range(GROUPS)] for r in range(RING)]
        bottom_landed = sem("bottom_landed")
        raw_landed = [sem(f"raw_landed{r}") for r in range(2)]
        wanted_landed = [sem(f"wanted_landed{r}") for r in range(2)]
        w1_landed = sem("w1_landed")
        w2_landed = sem("w2_landed")
        small_landed = sem("small_landed")
        row_number_landed = sem("row_number_landed")
        aside_landed = [sem(f"aside_landed{r}") for r in range(2)]
        out_landed = sem("out_landed")
        identity_zero = sem("identity_zero")
        identity_ready = sem("identity_ready")
        transposed = sem("transposed")
        grammed = sem("grammed")
        onehot_used = sem("onehot_used")
        accumulated = sem("accumulated")
        turned_out = sem("turned_out")
        act_regrouped = sem("act_regrouped")
        acc_out = sem("acc_out")
        table_high = sem("table_high")
        weights_high = sem("weights_high")
        dve_regrouped = sem("dve_regrouped")
        table_split = sem("table_split")
        onehot_ready = sem("onehot_ready")
        weights_split = sem("weights_split")
        cleared = sem("cleared")
        slot0_ready = sem("slot0_ready")
        bottom_high = sem("bottom_high")
        bottom_split = sem("bottom_split")
        pairs_high = sem("pairs_high")
        pairs_split = sem("pairs_split")
        h1_high = sem("h1_high")
        h1_split = sem("h1_split")
        gate = {name: sem(f"gate_{name}") for name in ("sp", "pool", "act", "dve")}

        PRIME_TRANSPOSED = RING * GROUPS
        PRIME_TURNED = 2
        PRIME_GRAMMED = BLOCK_TILES
        PRIME_REGROUPED = 2
        PRIME_PAIRS = 2
        PRIME_H1 = 2
        PRIME_OUT = 16
        MLP_FILLS = M1 + M2 + 1
        ACT_QUADRANTS = (2, 3, 3, 3)

        def fills_before(b):
            return b * (NH + MLP_FILLS) + NH

        def fills_before_round(r):
            return 0 if isinstance(r, int) and r == 0 else fills_before(r - 1)

        def at_least(eng, semaphore, count):
            if not (isinstance(count, int) and count <= 0):
                eng.wait_ge(semaphore, count)

        def gated(eng, name, semaphore, count):
            at_least(eng, semaphore, count)
            if not isinstance(count, int):
                eng.sem_inc(gate[name], 1)

        def block_of(t, b):
            return t[:, bass.ds(b * BLOCK, BLOCK)]

        block = ctx.enter_context(nc.Block())

        @block.sync
        def _(sp):
            def load_raw(r, i):
                at_least(sp, table_split, r * NH + (i - 1 if i >= 2 else 0))
                sp.dma_start(table_raw[0:ROW_PARTS, i % 2], onehot_tables[i].rearrange("(p c) d -> p c d", c=CHUNKS)
                             ).then_inc(raw_landed[i % 2], 16)

            def load_wanted(r, i):
                gated(sp, "sp", onehot_ready, (r * NH + (i - 1 if i >= 2 else 0)) * CHUNKS)
                sp.dma_start(wanted[:, i % 2, :], onehot_ids[i:i + 1, bass.ds(r * BLOCK, BLOCK)].to_broadcast([P, BLOCK])
                             ).then_inc(wanted_landed[i % 2], 16)

            def load_index(b, h):
                for r in range(RING):
                    for g in range(GROUPS):
                        gated(sp, "sp", rows_landed[r][g], 16 * SIZES[g] * (2 * (b - 1) + h + 1))
                sp.dma_start(index[h][:], ids[bass.ds(b, 1), h].rearrange("o p i -> (o p) i")).then_inc(
                    index_landed[h], 16)

            def move_aside(b, q):
                sp.wait_ge(act_regrouped, b * BLOCK_TILES + q + 1 + PRIME_REGROUPED)
                sp.wait_ge(dve_regrouped, b * BLOCK_TILES + q + 1 + PRIME_REGROUPED)
                row = FREE_ROW
                for c, columns, n in ASIDE_MOVES:
                    sp.dma_start(pairs[row:row + n, q % 2, 0:columns, :],
                                 aside[0:n, q % 2, c - 1:c - 1 + columns, :]).then_inc(aside_landed[q % 2], 16)
                    row += n

            sp.dma_start(index[0][:], ids[0, 0]).then_inc(index_landed[0], 16)
            load_wanted(0, 0)
            sp.dma_start(row_number[:], row_numbers).then_inc(row_number_landed, 16)
            load_raw(0, 1)
            load_wanted(0, 1)
            sp.dma_start(index[1][:], ids[0, 1]).then_inc(index_landed[1], 16)
            for i in range(2, NH):
                load_raw(0, i)
                load_wanted(0, i)
                if i == 2:
                    sp.dma_start(bottom[:], xT).then_inc(bottom_landed, 16)
            sp.dma_start(w1_raw, w1).then_inc(w1_landed, 16)
            sp.dma_start(w2_raw, w2).then_inc(w2_landed, 16)
            for to, of in ((b1_sb, b1), (b2_sb, b2), (w3_sb, w3)):
                sp.dma_start(to[:], of).then_inc(small_landed, 16)

            with sp.Fori(0, BLOCKS - 1) as b:
                for i in range(2):
                    load_raw(b + 1, i)
                    load_wanted(b + 1, i)
                load_index(b + 1, 0)
                move_aside(b, 0)
                move_aside(b, 1)
                load_raw(b + 1, 2)
                move_aside(b, 2)
                load_raw(b + 1, 3)
                move_aside(b, 3)
                load_index(b + 1, 1)
                for i in range(2, NH):
                    load_wanted(b + 1, i)
                    if i + 2 < NH:
                        load_raw(b + 1, i + 2)
            for q in range(BLOCK_TILES):
                move_aside(BLOCKS - 1, q)
            sp.wait_ge(out_landed, 16 * BLOCKS + PRIME_OUT)

        @block.gpsimd
        def _(pool):
            pool.memset(identity[:], 0.0).then_inc(identity_zero, 1)
            pool.wait_ge(identity_zero, 1)
            pool.affine_select(out=identity[:], in_=identity[:], compare_op=ALU.not_equal, fill=1.0,
                               base=0, pattern=[[-1, P]], channel_multiplier=1).then_inc(identity_ready, 1)
            with pool.Fori(0, BLOCKS) as b:
                for q in range(BLOCK_TILES):
                    if q % 2 == 0:
                        pool.wait_ge(index_landed[q // 2], b * 16 + 16)
                    for g in range(GROUPS):
                        if g == 0:
                            gated(pool, "pool", transposed, b * BLOCK_GROUPS + q * GROUPS + 2)
                        if g == 2:
                            gated(pool, "pool", transposed, b * BLOCK_GROUPS + (q + 1) * GROUPS)
                        for f in range(GROUP * g, GROUP * g + SIZES[g]):
                            at = (q % 2) * NG + f
                            pool.indirect_dma_start(
                                out=rows[:, q % RING, f, :], out_offset=None, in_=gathered[f],
                                in_offset=bass.IndirectOffsetOnAxis(ap=index[q // 2][:, at:at + 1], axis=0),
                            ).then_inc(rows_landed[q % RING][g], 16)

        TURN_SAMPLES = 16
        TURN_TABLE = NH - GROUPS - 1
        TURN_STEPS = (1, 3)

        @block.tensor
        def _(pe):
            pe.sem_inc(transposed, PRIME_TRANSPOSED)
            pe.sem_inc(grammed, PRIME_GRAMMED)

            def transpose_group(b, q, g):
                n = q * GROUPS + g
                pe.wait_ge(rows_landed[q % RING][g], 16 * SIZES[g] * (2 * b + q // 2 + 1))
                pe.wait_ge(turned_out, b * BLOCK_GROUPS + n - 1 + PRIME_TURNED)
                for i in range(SIZES[g]):
                    last = pe.transpose(turned[:, n % 2, i, :], rows[:, q % RING, GROUP * g + i, :], identity[:])
                last.then_inc(transposed, 1)

            def onehot_lookups(r, turn=None):
                for i in range(NH):
                    base = fills_before_round(r)
                    at_least(pe, acc_out, base if i == 0 else base + i - 1)
                    at_least(pe, table_split, r * NH + i + 1)
                    for c in range(CHUNKS):
                        at_least(pe, onehot_ready, (r * NH + i) * CHUNKS + c + 1)
                        pe.matmul(acc[:, i % 2, :], table_hi[0:ROW_PARTS, i % TABLE_RING, c, :], onehot[0:ROW_PARTS, c, :],
                                  start=(c == 0), stop=False)
                        last = pe.matmul(acc[:, i % 2, :], table_lo[0:ROW_PARTS, i % TABLE_RING, c, :],
                                         onehot[0:ROW_PARTS, c, :], start=False, stop=(c == CHUNKS - 1))
                        if c < CHUNKS - 1:
                            last.then_inc(onehot_used, 1)
                        if turn and c == CHUNKS // 2 and 0 <= i - TURN_TABLE < GROUPS:
                            turn(i - TURN_TABLE)
                    last.then_inc(accumulated, 1)

            def gram_tile(b, q, turn=None):
                pe.wait_ge(turned_out, b * BLOCK_GROUPS + (q + 1) * GROUPS + PRIME_TURNED)
                pe.wait_ge(act_regrouped, b * BLOCK_TILES + q - 1 + PRIME_REGROUPED)
                pe.wait_ge(dve_regrouped, b * BLOCK_TILES + q - 1 + PRIME_REGROUPED)
                for i in range(P):
                    at = QUADRANT * (i % 4)
                    last = pe.matmul(gram[at:at + GRAM, q % 2, i // 4, 0:GRAM],
                                     features[:, q, i, 0:GRAM], features[:, q, i, 1:SLOTS], start=True, stop=True)
                    if turn and (i + 1) % TURN_SAMPLES == 0 and (i + 1) // TURN_SAMPLES <= GROUPS:
                        turn((i + 1) // TURN_SAMPLES - 1)
                last.then_inc(grammed, 1)

            def product(to, w_hi, w_lo, x_hi, x_lo, first, last):
                pe.matmul(to, w_hi, x_hi, start=first, stop=False)
                pe.matmul(to, w_hi, x_lo, start=False, stop=False)
                return pe.matmul(to, w_lo, x_hi, start=False, stop=last)

            def mlp(b, fill, base, turn=None):
                pe.wait_ge(bottom_split, b + 1)
                for m in range(M1):
                    pe.wait_ge(acc_out, base + max(fill - 1, 0))
                    to = acc[:, fill % 2, :]
                    at = slice(m * P, (m + 1) * P)
                    for step, k in enumerate((PAIR_TILES, *range(PAIR_TILES))):
                        if k == 0 and m == 0:
                            pe.wait_ge(pairs_split, b * BLOCK_TILES + BLOCK_TILES + PRIME_PAIRS)
                        x_hi, x_lo = ((bottom_hi[:], bottom_lo[:]) if k == PAIR_TILES
                                      else (pairs_hi[:, k, :], pairs_lo[:, k, :]))
                        last = product(to, w1_hi[:, k, at], w1_lo[:, k, at], x_hi, x_lo,
                                       k == PAIR_TILES, k == PAIR_TILES - 1)
                        if turn and step in TURN_STEPS and m * len(TURN_STEPS) + TURN_STEPS.index(step) < GROUPS:
                            turn(m * len(TURN_STEPS) + TURN_STEPS.index(step))
                    last.then_inc(accumulated, 1)
                    fill += 1

                pe.wait_ge(acc_out, base + fill)
                at = [slice(m * P, (m + 1) * P) for m in range(M2)]
                for k, m in [(k, m) for ks in (range(M1 - 1), (M1 - 1,)) for m in range(M2) for k in ks]:
                    if m == 0:
                        pe.wait_ge(h1_split, b * M1 + k + 1 + PRIME_H1)
                    last = product(acc[:, (fill + m) % 2, :], w2_hi[:, k, at[m]], w2_lo[:, k, at[m]],
                                   h1_hi[:, k, :], h1_lo[:, k, :], k == 0, k == M1 - 1)
                    if k == M1 - 1:
                        last.then_inc(accumulated, 1)
                fill += M2

            def output_layer(b, fill, base):
                pe.wait_ge(acc_out, base + fill)
                for k in range(M2):
                    last = pe.matmul(acc[0:1, fill % 2, :], w3_sb[:, k:k + 1], h2[:, k, :],
                                     start=(k == 0), stop=(k == M2 - 1))
                last.then_inc(accumulated, 1)

            def first_gram(b, after_group1=None):
                def between(g):
                    transpose_group(b, 2, g)
                    if g == 1 and after_group1:
                        after_group1()

                pe.wait_ge(slot0_ready, b + 1)
                gram_tile(b, 0, between)

            def block_steps(b, more):
                gram_tile(b, 1, lambda g: transpose_group(b, 3, g))
                gram_tile(b, 2)
                gram_tile(b, 3)
                if more:
                    onehot_lookups(b + 1, lambda g: transpose_group(b, BLOCK_TILES, g))
                    mlp(b, NH, fills_before(b), lambda g: transpose_group(b, BLOCK_TILES + 1, g))
                    first_gram(b + 1, lambda: output_layer(b, NH + MLP_FILLS - 1, fills_before(b)))
                else:
                    mlp(b, 0, fills_before(b))
                    output_layer(b, MLP_FILLS - 1, fills_before(b))

            onehot_lookups(0)
            pe.wait_ge(identity_ready, 1)
            for q in range(2):
                for g in range(GROUPS):
                    transpose_group(0, q, g)
            pe.wait_ge(acc_out, NH)
            pe.wait_ge(cleared, 1)
            pe.wait_ge(weights_split, 2)
            first_gram(0)
            with pe.Fori(0, BLOCKS - 1) as b:
                block_steps(b, True)
            block_steps(BLOCKS - 1, False)

        def regroup(copy, q, quadrants):
            for s in quadrants:
                def of(n, c, columns):
                    return gram[QUADRANT * s:QUADRANT * s + n, q % 2, :, c - 1:c - 1 + columns].rearrange(
                        "f t k -> f k t")

                def to(t, start, n, columns):
                    return t[start:start + n, q % 2, 0:columns, :].rearrange("f k (t s) -> f s k t", s=4)[:, s]

                copy(to(aside, 0, ASIDE, ASIDE), of(ASIDE, 1, ASIDE))
                for j in range(4):
                    last = copy(to(pairs, QUADRANT * j, COLUMN_ROWS[j], PAIR_TILES),
                                of(COLUMN_ROWS[j], COLUMNS_FROM[j], PAIR_TILES))
            return last

        @block.scalar
        def _(act):
            act.sem_inc(turned_out, PRIME_TURNED)
            act.sem_inc(act_regrouped, PRIME_REGROUPED)
            act.sem_inc(out_landed, PRIME_OUT)

            def turned_group(b, q, g):
                if g == 0:
                    act.wait_ge(grammed, b * BLOCK_TILES + q + 1 - BLOCK_TILES + PRIME_GRAMMED)
                n = q * GROUPS + g
                act.wait_ge(transposed, b * BLOCK_GROUPS + n + 1 + PRIME_TRANSPOSED)
                at = 1 + GROUP * g
                nc.scalar.copy(features[:, q % BLOCK_TILES, :, at:at + SIZES[g]].rearrange("d b f -> d f b"),
                               turned[:, n % 2, 0:SIZES[g], :]).then_inc(turned_out, 1)

            def turned_tile(b, q):
                for g in range(GROUPS):
                    turned_group(b, q, g)

            def regroup_tile(b, q):
                act.wait_ge(grammed, b * BLOCK_TILES + q + 1 + PRIME_GRAMMED)
                act.wait_ge(pairs_split, b * BLOCK_TILES + q - 1 + PRIME_PAIRS)
                regroup(nc.scalar.copy, q, range(ACT_QUADRANTS[q])).then_inc(act_regrouped, 1)

            def table_high_part(r, i):
                uses = (NH + 1 - i % 2) // 2
                act.wait_ge(raw_landed[i % 2], 16 * (r * uses + i // 2 + 1))
                if i >= TABLE_RING:
                    act.wait_ge(accumulated, fills_before_round(r) + i + 1 - TABLE_RING)
                nc.scalar.copy(table_hi[0:ROW_PARTS, i % TABLE_RING], table_raw[0:ROW_PARTS, i % 2]).then_inc(
                    table_high, 1)

            def onehot_out(r, turned_of=None):
                for i in range(NH):
                    if turned_of and 0 <= i - TURN_TABLE < GROUPS:
                        turned_of(i - TURN_TABLE)
                    act.wait_ge(accumulated, fills_before_round(r) + i + 1)
                    nc.scalar.copy(features[:, :, :, 1 + NG + i].rearrange("d q b -> d (q b)"),
                                   acc[:, i % 2, :]).then_inc(acc_out, 1)
                    if i + TABLE_RING < NH:
                        table_high_part(r, i + TABLE_RING)

            def mlp_out(b, fill, base, turned_of=None):
                for m in range(M1):
                    if turned_of:
                        for g in range(m * len(TURN_STEPS), min((m + 1) * len(TURN_STEPS), GROUPS)):
                            turned_of(g)
                    act.wait_ge(accumulated, base + fill + 1)
                    act.wait_ge(h1_split, b * M1 + m - 1 + PRIME_H1)
                    nc.scalar.activation(h1[:, m % 2, :], acc[:, fill % 2, :], ACT.Relu,
                                         bias=b1_sb[:, m:m + 1]).then_inc(acc_out, 1)
                    fill += 1
                for m in range(M2):
                    act.wait_ge(accumulated, base + fill + 1)
                    nc.scalar.activation(h2[:, m, :], acc[:, fill % 2, :], ACT.Relu,
                                         bias=b2_sb[:, m:m + 1]).then_inc(acc_out, 1)
                    fill += 1

            def output(b, fill, base):
                act.wait_ge(accumulated, base + fill + 1)
                act.wait_ge(out_landed, 16 * b + PRIME_OUT)
                nc.scalar.copy(y_sb[:], acc[0:1, fill % 2, :]).then_inc(acc_out, 1)
                gated(act, "act", acc_out, base + fill + 1)
                act.dma_start(out[:, bass.ds(b * BLOCK, BLOCK)], y_sb[:]).then_inc(out_landed, 16)

            def block_steps(b, more):
                for q in range(BLOCK_TILES):
                    regroup_tile(b, q)
                    if q == 0:
                        turned_tile(b, 3)
                    if more and q < TABLE_RING:
                        table_high_part(b + 1, q)
                if more:
                    onehot_out(b + 1, lambda g: turned_group(b, BLOCK_TILES, g))
                    mlp_out(b, NH, fills_before(b), lambda g: turned_group(b, BLOCK_TILES + 1, g))
                    for g in range(GROUPS):
                        turned_group(b + 1, 2, g)
                        if g == 1:
                            output(b, NH + MLP_FILLS - 1, fills_before(b))
                else:
                    mlp_out(b, 0, fills_before(b))
                    output(b, MLP_FILLS - 1, fills_before(b))

            act.dma_start(table_raw[0:ROW_PARTS, 0], onehot_tables[0].rearrange("(p c) d -> p c d", c=CHUNKS)
                          ).then_inc(raw_landed[0], 16)
            for i in range(TABLE_RING):
                table_high_part(0, i)
            onehot_out(0)
            turned_tile(0, 0)
            act.wait_ge(w1_landed, 16)
            nc.scalar.copy(w1_hi[:], w1_raw).then_inc(weights_high, 1)
            act.wait_ge(w2_landed, 16)
            nc.scalar.copy(w2_hi[:], w2_raw).then_inc(weights_high, 1)
            turned_tile(0, 1)
            act.wait_ge(small_landed, 3 * 16)
            act.wait_ge(cleared, 1)
            act.wait_ge(weights_split, 2)
            turned_tile(0, 2)
            with act.Fori(0, BLOCKS - 1) as b:
                block_steps(b, True)
            block_steps(BLOCKS - 1, False)

        @block.vector
        def _(dve):
            dve.sem_inc(dve_regrouped, PRIME_REGROUPED)
            dve.sem_inc(pairs_split, PRIME_PAIRS)
            dve.sem_inc(h1_split, PRIME_H1)

            def table_low_part(r, i):
                dve.wait_ge(table_high, r * NH + i + 1)
                dve.tensor_tensor(table_lo[0:ROW_PARTS, i % TABLE_RING], table_raw[0:ROW_PARTS, i % 2],
                                  table_hi[0:ROW_PARTS, i % TABLE_RING], ALU.subtract).then_inc(table_split, 1)

            def onehot_chunk(r, i, c):
                if c == 0:
                    uses = (NH + 1 - i % 2) // 2
                    dve.wait_ge(wanted_landed[i % 2], 16 * (r * uses + i // 2 + 1))
                if i >= 1:
                    if c < CHUNKS - 1:
                        dve.wait_ge(onehot_used, (r * NH + i - 1) * (CHUNKS - 1) + c + 1)
                    else:
                        dve.wait_ge(accumulated, fills_before_round(r) + i)
                dve.tensor_scalar(onehot[0:ROW_PARTS, c, :], wanted[0:ROW_PARTS, i % 2, :],
                                  row_number[0:ROW_PARTS, c:c + 1], None, ALU.is_equal).then_inc(onehot_ready, 1)

            def onehots(r, i):
                if i >= TABLE_RING:
                    table_low_part(r, i)
                for c in range(CHUNKS):
                    onehot_chunk(r, i, c)

            def fill_slot0(b):
                gated(dve, "dve", slot0_ready, b)
                dve.tensor_copy(features[:, :, :, 0].rearrange("d q b -> d (q b)"), block_of(bottom, b)).then_inc(
                    slot0_ready, 1)

            def split_bottom(b):
                gated(dve, "dve", bottom_split, b)
                dve.tensor_copy(bottom_hi[:], block_of(bottom, b)).then_inc(bottom_high, 1)
                gated(dve, "dve", bottom_high, b + 1)
                dve.tensor_tensor(bottom_lo[:], block_of(bottom, b), bottom_hi[:], ALU.subtract).then_inc(bottom_split, 1)

            def regroup_tile(b, q):
                dve.wait_ge(grammed, b * BLOCK_TILES + q + 1 + PRIME_GRAMMED)
                dve.wait_ge(pairs_split, b * BLOCK_TILES + q - 1 + PRIME_PAIRS)
                regroup(dve.tensor_copy, q, range(ACT_QUADRANTS[q], 4)).then_inc(dve_regrouped, 1)

            def split_tile(b, q):
                dve.wait_ge(act_regrouped, b * BLOCK_TILES + q + 1 + PRIME_REGROUPED)
                dve.wait_ge(dve_regrouped, b * BLOCK_TILES + q + 1 + PRIME_REGROUPED)
                dve.wait_ge(aside_landed[q % 2], 16 * len(ASIDE_MOVES) * (2 * b + q // 2 + 1))
                at = slice(q * P, (q + 1) * P)
                dve.tensor_copy(pairs_hi[:, :, at], pairs[:, q % 2]).then_inc(pairs_high, 1)
                dve.wait_ge(pairs_high, b * BLOCK_TILES + q + 1)
                dve.tensor_tensor(pairs_lo[:, :, at], pairs[:, q % 2], pairs_hi[:, :, at],
                                  ALU.subtract).then_inc(pairs_split, 1)

            def block_steps(b, more):
                for q in range(BLOCK_TILES):
                    regroup_tile(b, q)
                    if more:
                        for c in (2 * q, 2 * q + 1):
                            onehot_chunk(b + 1, 0, c)
                    if more and q:
                        table_low_part(b + 1, q - 1)
                    if q:
                        split_tile(b, q - 1)
                if more:
                    for i in range(1, NH):
                        onehots(b + 1, i)
                        if i == SPLIT_AFTER:
                            split_tile(b, BLOCK_TILES - 1)
                else:
                    split_tile(b, BLOCK_TILES - 1)
                for m in range(M1):
                    dve.wait_ge(acc_out, fills_before(b) + (NH if more else 0) + m + 1)
                    dve.tensor_copy(h1_hi[:, m, :], h1[:, m % 2, :]).then_inc(h1_high, 1)
                    dve.wait_ge(h1_high, b * M1 + m + 1)
                    dve.tensor_tensor(h1_lo[:, m, :], h1[:, m % 2, :], h1_hi[:, m, :],
                                      ALU.subtract).then_inc(h1_split, 1)
                if more:
                    fill_slot0(b + 1)
                    split_bottom(b + 1)

            SPLIT_AFTER = 4
            dve.memset(pairs[:], 0.0).then_inc(cleared, 1)
            dve.wait_ge(row_number_landed, 16)
            onehots(0, 0)
            for i in range(TABLE_RING):
                table_low_part(0, i)
                if i:
                    onehots(0, i)
            for i in range(TABLE_RING, NH):
                onehots(0, i)
            dve.wait_ge(bottom_landed, 16)
            fill_slot0(0)
            split_bottom(0)
            dve.wait_ge(weights_high, 2)
            dve.tensor_tensor(w1_lo[:], w1_raw, w1_hi[:], ALU.subtract).then_inc(weights_split, 1)
            dve.tensor_tensor(w2_lo[:], w2_raw, w2_hi[:], ALU.subtract).then_inc(weights_split, 1)
            dve.wait_ge(weights_split, 2)
            dve.wait_ge(cleared, 1)
            with dve.Fori(0, BLOCKS - 1) as b:
                block_steps(b, True)
            block_steps(BLOCKS - 1, False)


def layer1_rows():
    import numpy as np

    feature = [0] + [1 + t for t in SLOT_TABLES]
    number = {}
    for f in range(SLOTS):
        for g in range(f + 1, SLOTS):
            number[f, g] = number[g, f] = len(number) // 2

    at = np.full((P, PAIR_TILES), -1)
    for k in range(PAIR_TILES):
        for j in range(4):
            g = COLUMNS_FROM[j] + k
            for f in range(g):
                at[QUADRANT * j + f, k] = number[feature[f], feature[g]]
        row = FREE_ROW
        for c, columns, n in ASIDE_MOVES:
            if k < columns:
                for f in range(c + k):
                    at[row + f, k] = number[feature[f], feature[c + k]]
            row += n
    return at, len(number) // 2


def kernel(**inputs):
    import numpy as np
    import concourse.bacc as bacc
    from concourse.bass_utils import run_bass_kernel_spmd

    a = {name: np.asarray(v) for name, v in inputs.items()}
    at, pairs = layer1_rows()
    w1 = np.zeros((P, K1, HIDDEN1), np.float32)
    w1[:, :PAIR_TILES][at >= 0] = a["W_top1"][at[at >= 0]]
    w1[:, PAIR_TILES] = a["W_top1"][pairs:]
    arrays = {
        "in_xT": a["r_bottom_output"].T,
        "in_ids": a["ids"][:, GATHERED].reshape(BLOCKS, 2, 2, P, NG).transpose(0, 1, 3, 2, 4).reshape(BLOCKS, 2, P, 2 * NG),
        "in_onehot_ids": a["ids"][:, ONEHOT].T,
        "in_row_numbers": np.arange(P * CHUNKS, dtype=np.float32).reshape(P, CHUNKS),
        "in_w1": w1,
        "in_b1": a["b_top1"].reshape(M1, P).T,
        "in_w2": a["W_top2"].reshape(M1, P, HIDDEN2).transpose(1, 0, 2),
        "in_b2": a["b_top2"].reshape(M2, P).T,
        "in_w3": a["W_top3"].reshape(M2, P).T,
    }
    for f in range(TABLES):
        arrays[f"in_tbl_{f}"] = a[f"tbl_{f}"]
    arrays = {name: np.ascontiguousarray(x) for name, x in arrays.items()}

    nc = bacc.Bacc("TRN2", target_bir_lowering=False, num_devices=1)
    ap = {name: nc.dram_tensor(name, x.shape, mybir.dt.from_np(x.dtype), kind="ExternalInput").ap()
          for name, x in arrays.items()}
    out = nc.dram_tensor("out", (BATCH, 1), F32, kind="ExternalOutput").ap()
    dlrm_tower(nc, ap["in_xT"], ap["in_ids"], ap["in_onehot_ids"], ap["in_row_numbers"],
               [ap[f"in_tbl_{f}"] for f in GATHERED], [ap[f"in_tbl_{f}"] for f in ONEHOT],
               ap["in_w1"], ap["in_b1"], ap["in_w2"], ap["in_b2"], ap["in_w3"],
               out.rearrange("n o -> o n"))
    r = run_bass_kernel_spmd(nc, [arrays], core_ids=[0])
    return r.results[0]["out"]
```

```python
from contextlib import ExitStack

import concourse.bass as bass
from concourse import mybir

P = 128
D = 128
BATCH = 2048
TABLES = 26
SLOTS = TABLES + 1
BLOCK_TILES = 4
BLOCKS = BATCH // (P * BLOCK_TILES)
TILES = BLOCKS * BLOCK_TILES
BLOCK = P * BLOCK_TILES
HIDDEN1, HIDDEN2 = 512, 256
M1, M2 = HIDDEN1 // P, HIDDEN2 // P

ONEHOT = [3, 4, 9, 13, 14, 17, 20, 21]
ONEHOT_ROWS = 1000
CHUNKS = 8
ACT_CHUNK = 5
ROW_PARTS = ONEHOT_ROWS // CHUNKS
NH = len(ONEHOT)
GATHERED = [f for f in range(TABLES) if f not in ONEHOT]
NG = len(GATHERED)
SLOT_TABLES = GATHERED + ONEHOT

EXTRA = 4
EXTRA_TILES = 3
EXTRA_SAMPLES = P * EXTRA_TILES
FIRST_ONEHOT = ONEHOT + GATHERED[NG - EXTRA:]

GROUP = 4
GROUPS = -(-NG // GROUP)
SIZES = [min(GROUP, NG - GROUP * g) for g in range(GROUPS)]
BLOCK_GROUPS = BLOCK_TILES * GROUPS
LEFT = NG - EXTRA
FIRST_SIZES = [GROUP] * (GROUPS - 2) + [LEFT - GROUP * (GROUPS - 2) - 1, 1]
assert all(0 < n <= m for n, m in zip(FIRST_SIZES, SIZES))
RING = 2

QUADRANT = 32
GRAM = SLOTS - 1
TABLE_RING = 4
TABLES_AHEAD = TABLE_RING - 1

COLUMNS_FROM = [15, 19, 23, 11]
PAIR_TILES = 4
COLUMN_ROWS = [c + PAIR_TILES - 1 for c in COLUMNS_FROM]
ASIDE = 10
ASIDE_MOVES = [(7, 4, 10), (3, 4, 6), (1, 2, 2)]
FREE_ROW = QUADRANT * 3 + COLUMN_ROWS[3]
assert FREE_ROW + sum(n for _, _, n in ASIDE_MOVES) == P
K1 = PAIR_TILES + 1

F32 = mybir.dt.float32
F32R = mybir.dt.float32r
I32 = mybir.dt.int32
ALU = mybir.AluOpType
ACT = mybir.ActivationFunctionType


def dlrm_tower(nc, xT, ids, onehot_ids, row_numbers, gathered, onehot_tables, w1, b1, w2, b2, w3, out):
    with ExitStack() as ctx:
        def sb(name, shape, dt=F32):
            return ctx.enter_context(nc.sbuf_tensor(name, shape, dt))

        def psum(name, shape):
            return ctx.enter_context(nc.psum_tensor(name, shape, F32))

        def sem(name):
            return ctx.enter_context(nc.semaphore(name))

        identity = sb("identity", [P, P])
        index = [sb(f"index{h}", [P, 2 * NG], I32) for h in range(2)]
        rows = sb("rows", [P, RING, NG, D])
        features = sb("features", [P, BLOCK_TILES, P, SLOTS])
        bottom = sb("bottom", [P, BLOCK])
        bottom_hi = sb("bottom_hi", [P, BLOCK], F32R)
        bottom_lo = sb("bottom_lo", [P, BLOCK], F32R)
        row_number = sb("row_number", [P, CHUNKS + 2])
        distance = sb("distance", [P, BLOCK])
        table_raw = sb("table_raw", [P, 2, CHUNKS, D])
        table_hi = sb("table_hi", [P, TABLE_RING, CHUNKS, D], F32R)
        table_lo = sb("table_lo", [P, TABLE_RING, CHUNKS, D], F32R)
        wanted = sb("wanted", [P, 2, BLOCK], I32)
        pairs = sb("pairs", [P, 2, PAIR_TILES, P])
        aside = sb("aside", [P, 2, ASIDE, P])
        pairs_hi = sb("pairs_hi", [P, PAIR_TILES, BLOCK], F32R)
        pairs_lo = sb("pairs_lo", [P, PAIR_TILES, BLOCK], F32R)
        w1_hi = sb("w1_hi", [P, K1, HIDDEN1], F32R)
        w1_lo = sb("w1_lo", [P, K1, HIDDEN1], F32R)
        w2_hi = sb("w2_hi", [P, M1, HIDDEN2], F32R)
        w2_lo = sb("w2_lo", [P, M1, HIDDEN2], F32R)
        b1_sb = sb("b1_sb", [P, M1])
        b2_sb = sb("b2_sb", [P, M2])
        w3_sb = sb("w3_sb", [P, M2])
        h1 = sb("h1", [P, 2, BLOCK])
        y_sb = sb("y_sb", [1, BLOCK])
        onehot = sb("onehot", [P, CHUNKS, BLOCK], F32R)
        h1_hi = onehot[:, 0:M1]
        h1_lo = onehot[:, M1:2 * M1]
        h2 = aside[:, 1].rearrange("p c n -> p (c n)")[:, 0:M2 * BLOCK].rearrange("p (m n) -> p m n", m=M2)
        w1_raw = aside[:].rearrange("p r c n -> p (r c n)").rearrange("p (k n) -> p k n", k=K1)
        w2_raw = h1[:].rearrange("p r n -> p (r n)").rearrange("p (k n) -> p k n", k=M1)

        turned = psum("turned", [P, 2, GROUP, P])
        gram = psum("gram", [P, 2, P // 4, QUADRANT])
        acc = psum("acc", [P, 2, BLOCK])

        index_landed = [sem(f"index_landed{h}") for h in range(2)]
        rows_landed = [[sem(f"rows_landed{r}_{g}") for g in range(GROUPS)] for r in range(RING)]
        bottom_landed = sem("bottom_landed")
        raw_landed = [sem(f"raw_landed{r}") for r in range(2)]
        wanted_landed = [sem(f"wanted_landed{r}") for r in range(2)]
        w1_landed = sem("w1_landed")
        w2_landed = sem("w2_landed")
        small_landed = sem("small_landed")
        row_number_landed = sem("row_number_landed")
        aside_landed = [sem(f"aside_landed{r}") for r in range(2)]
        out_landed = sem("out_landed")
        identity_zero = sem("identity_zero")
        identity_ready = sem("identity_ready")
        transposed = sem("transposed")
        grammed = sem("grammed")
        onehot_used = sem("onehot_used")
        accumulated = sem("accumulated")
        turned_out = sem("turned_out")
        act_regrouped = sem("act_regrouped")
        acc_out = sem("acc_out")
        table_high = sem("table_high")
        distance_ready = sem("distance_ready")
        act_chunk_ready = sem("act_chunk_ready")
        weights_high = sem("weights_high")
        dve_regrouped = sem("dve_regrouped")
        table_split = sem("table_split")
        onehot_ready = sem("onehot_ready")
        weights_split = sem("weights_split")
        cleared = sem("cleared")
        slot0_ready = sem("slot0_ready")
        bottom_high = sem("bottom_high")
        bottom_split = sem("bottom_split")
        pairs_high = sem("pairs_high")
        pairs_split = sem("pairs_split")
        h1_high = sem("h1_high")
        h1_split = sem("h1_split")
        gate = {name: sem(f"gate_{name}") for name in ("sp", "pool", "act")}

        PRIME_TRANSPOSED = RING * GROUPS
        PRIME_TURNED = 2
        PRIME_GRAMMED = BLOCK_TILES
        PRIME_REGROUPED = 2
        PRIME_PAIRS = 2
        PRIME_H1 = 2
        PRIME_OUT = 16
        MLP_FILLS = M1 + M2 + 1
        ACT_QUADRANTS = (2, 3, 3, 3)
        HIGH_PARTS = ((0,), (1,), (2,))
        LAST_ACT_QUADRANTS = 2

        def fills_before(b):
            return b * (NH + MLP_FILLS) + NH + EXTRA

        def fills_before_round(r):
            return 0 if isinstance(r, int) and r == 0 else fills_before(r - 1)

        def tables_of(r):
            return NH + EXTRA if isinstance(r, int) and r == 0 else NH

        def tables_before(r):
            return 0 if isinstance(r, int) and r == 0 else r * NH + EXTRA

        def landed(r, i):
            half = i % 2
            before = 0 if isinstance(r, int) and r == 0 else r * ((NH + 1 - half) // 2) + (EXTRA + 1 - half) // 2
            return 16 * (before + i // 2 + 1)

        def samples_of(r, i):
            return slice(0, BLOCK if i < NH else EXTRA_SAMPLES)

        def group_of(b, q, g):
            first = isinstance(b, int) and b == 0 and q < EXTRA_TILES
            sizes = FIRST_SIZES if first else SIZES
            return sum(sizes[:g]), sizes[g]

        def rows_count(b, q, g):
            if isinstance(b, int) and b == 0 and q < EXTRA_TILES:
                return 16 * FIRST_SIZES[g] * (q // 2 + 1)
            short = len(range(q % 2, EXTRA_TILES, 2))
            return 16 * (SIZES[g] * (2 * b + q // 2 + 1) - short * (SIZES[g] - FIRST_SIZES[g]))

        def at_least(eng, semaphore, count):
            if not (isinstance(count, int) and count <= 0):
                eng.wait_ge(semaphore, count)

        def gated(eng, name, semaphore, count):
            at_least(eng, semaphore, count)
            if not isinstance(count, int):
                eng.sem_inc(gate[name], 1)

        block = ctx.enter_context(nc.Block())

        @block.sync
        def _(sp):
            def load_raw(r, i):
                at_least(sp, table_split, tables_before(r) + (i - 1 if i >= 2 else 0))
                sp.dma_start(table_raw[0:ROW_PARTS, i % 2], onehot_tables[i].rearrange("(p c) d -> p c d", c=CHUNKS)
                             ).then_inc(raw_landed[i % 2], 16)

            def load_wanted(r, i):
                used = tables_before(r) + (i - 1 if i >= 2 else 0)
                gated(sp, "sp", onehot_ready, used * (CHUNKS - 1))
                gated(sp, "sp", act_chunk_ready, used)
                sp.dma_start(wanted[:, i % 2, :], onehot_ids[i:i + 1, bass.ds(r * BLOCK, BLOCK)].to_broadcast([P, BLOCK])
                             ).then_inc(wanted_landed[i % 2], 16)

            def load_bottom(b):
                gated(sp, "sp", bottom_split, b)
                sp.dma_start(bottom[:], xT[:, bass.ds(b * BLOCK, BLOCK)]).then_inc(bottom_landed, 16)

            def load_index(b, h):
                gated(sp, "sp", transposed, (b - 1) * BLOCK_GROUPS + (2 * h + 2) * GROUPS + PRIME_TRANSPOSED)
                sp.dma_start(index[h][:], ids[bass.ds(b, 1), h].rearrange("o p i -> (o p) i")).then_inc(
                    index_landed[h], 16)

            def move_aside(b, q):
                sp.wait_ge(act_regrouped, b * BLOCK_TILES + q + 1 + PRIME_REGROUPED)
                sp.wait_ge(dve_regrouped, b * BLOCK_TILES + q + 1 + PRIME_REGROUPED)
                row = FREE_ROW
                for c, columns, n in ASIDE_MOVES:
                    sp.dma_start(pairs[row:row + n, q % 2, 0:columns, :],
                                 aside[0:n, q % 2, c - 1:c - 1 + columns, :]).then_inc(aside_landed[q % 2], 16)
                    row += n

            sp.dma_start(index[0][:], ids[0, 0]).then_inc(index_landed[0], 16)
            load_wanted(0, 0)
            sp.dma_start(row_number[:], row_numbers).then_inc(row_number_landed, 16)
            load_raw(0, 1)
            load_wanted(0, 1)
            sp.dma_start(index[1][:], ids[0, 1]).then_inc(index_landed[1], 16)
            load_raw(0, 2)
            load_wanted(0, 2)
            load_raw(0, 3)
            for i in range(3, NH + EXTRA):
                load_wanted(0, i)
                if i == 3:
                    load_raw(0, 4)
                if i + 2 < NH + EXTRA:
                    load_raw(0, i + 2)
                if i == NH - 2:
                    load_bottom(0)
                if i == NH - 1:
                    sp.dma_start(w1_raw, w1).then_inc(w1_landed, 16)
                if i == NH:
                    sp.dma_start(w2_raw, w2).then_inc(w2_landed, 16)
                    for to, of in ((b1_sb, b1), (b2_sb, b2), (w3_sb, w3)):
                        sp.dma_start(to[:], of).then_inc(small_landed, 16)

            with sp.Fori(0, BLOCKS - 1) as b:
                for i in range(2):
                    load_raw(b + 1, i)
                    load_wanted(b + 1, i)
                load_index(b + 1, 0)
                load_bottom(b + 1)
                move_aside(b, 0)
                move_aside(b, 1)
                load_raw(b + 1, 2)
                load_raw(b + 1, 3)
                load_wanted(b + 1, 2)
                move_aside(b, 2)
                load_raw(b + 1, 4)
                load_wanted(b + 1, 3)
                load_raw(b + 1, 5)
                load_wanted(b + 1, 4)
                move_aside(b, 3)
                load_raw(b + 1, 6)
                load_index(b + 1, 1)
                for i in range(5, NH):
                    load_wanted(b + 1, i)
                    if i + 2 < NH:
                        load_raw(b + 1, i + 2)
            for q in range(BLOCK_TILES):
                move_aside(BLOCKS - 1, q)
            sp.wait_ge(out_landed, 16 * BLOCKS + PRIME_OUT)

        @block.gpsimd
        def _(pool):
            pool.memset(identity[:], 0.0).then_inc(identity_zero, 1)
            pool.wait_ge(identity_zero, 1)
            pool.affine_select(out=identity[:], in_=identity[:], compare_op=ALU.not_equal, fill=1.0,
                               base=0, pattern=[[-1, P]], channel_multiplier=1).then_inc(identity_ready, 1)

            def look_up_tile(b, q):
                if q % 2 == 0:
                    pool.wait_ge(index_landed[q // 2], b * 16 + 16)
                for g in range(GROUPS):
                    if g == 0:
                        gated(pool, "pool", transposed, b * BLOCK_GROUPS + q * GROUPS + 2)
                    if g == 2:
                        gated(pool, "pool", transposed, b * BLOCK_GROUPS + (q + 1) * GROUPS)
                    first, n = group_of(b, q, g)
                    for f in range(first, first + n):
                        at = (q % 2) * NG + f
                        pool.indirect_dma_start(
                            out=rows[:, q % RING, f, :], out_offset=None, in_=gathered[f],
                            in_offset=bass.IndirectOffsetOnAxis(ap=index[q // 2][:, at:at + 1], axis=0),
                        ).then_inc(rows_landed[q % RING][g], 16)

            for q in range(BLOCK_TILES):
                look_up_tile(0, q)
            with pool.Fori(1, BLOCKS) as b:
                for q in range(BLOCK_TILES):
                    look_up_tile(b, q)

        TURN_SAMPLES = 16
        TURN_TABLE = NH - GROUPS - 1
        TURN_STEPS = [(0, 1), (0, 3), (1, 1)]
        FIRST_TURNS = {NH + EXTRA - 2 * GROUPS + n: (n // GROUPS, n % GROUPS) for n in range(2 * GROUPS)}
        TURNS = {TURN_TABLE + g: (BLOCK_TILES, g) for g in range(GROUPS)}

        @block.tensor
        def _(pe):
            pe.sem_inc(transposed, PRIME_TRANSPOSED)
            pe.sem_inc(grammed, PRIME_GRAMMED)

            def transpose_group(b, q, g):
                n = q * GROUPS + g
                pe.wait_ge(rows_landed[q % RING][g], rows_count(b, q, g))
                pe.wait_ge(turned_out, b * BLOCK_GROUPS + n - 1 + PRIME_TURNED)
                first, size = group_of(b, q, g)
                for i in range(size):
                    last = pe.transpose(turned[:, n % 2, i, :], rows[:, q % RING, first + i, :], identity[:])
                last.then_inc(transposed, 1)

            def onehot_lookups(r):
                for i in range(tables_of(r)):
                    base = fills_before_round(r)
                    at_least(pe, acc_out, base if i == 0 else base + i - 1)
                    at_least(pe, table_split, tables_before(r) + i + 1)
                    samples = samples_of(r, i)
                    for c in range(CHUNKS):
                        if c != ACT_CHUNK:
                            pe.wait_ge(onehot_ready, (tables_before(r) + i) * (CHUNKS - 1) + c
                                       + (1 if c < ACT_CHUNK else 0))
                        else:
                            pe.wait_ge(act_chunk_ready, tables_before(r) + i + 1)
                        to, of = acc[:, i % 2, samples], onehot[0:ROW_PARTS, c, samples]
                        pe.matmul(to, table_hi[0:ROW_PARTS, i % TABLE_RING, c, :], of, start=(c == 0), stop=False)
                        last = pe.matmul(to, table_lo[0:ROW_PARTS, i % TABLE_RING, c, :], of,
                                         start=False, stop=(c == CHUNKS - 1))
                        if c < CHUNKS - 1:
                            last.then_inc(onehot_used, 1)
                        if c == CHUNKS // 2:
                            if isinstance(r, int):
                                if i in FIRST_TURNS:
                                    transpose_group(0, *FIRST_TURNS[i])
                            elif i in TURNS:
                                transpose_group(r - 1, *TURNS[i])
                    last.then_inc(accumulated, 1)

            def gram_tile(b, q, turn=None):
                pe.wait_ge(turned_out, b * BLOCK_GROUPS + (q + 1) * GROUPS + PRIME_TURNED)
                pe.wait_ge(act_regrouped, b * BLOCK_TILES + q - 1 + PRIME_REGROUPED)
                pe.wait_ge(dve_regrouped, b * BLOCK_TILES + q - 1 + PRIME_REGROUPED)
                for i in range(P):
                    at = QUADRANT * (i % 4)
                    last = pe.matmul(gram[at:at + GRAM, q % 2, i // 4, 0:GRAM],
                                     features[:, q, i, 0:GRAM], features[:, q, i, 1:SLOTS], start=True, stop=True)
                    if turn and (i + 1) % TURN_SAMPLES == 0 and (i + 1) // TURN_SAMPLES <= GROUPS:
                        turn((i + 1) // TURN_SAMPLES - 1)
                last.then_inc(grammed, 1)

            def product(to, w_hi, w_lo, x_hi, x_lo, first, last):
                pe.matmul(to, w_hi, x_hi, start=first, stop=False)
                pe.matmul(to, w_hi, x_lo, start=False, stop=False)
                return pe.matmul(to, w_lo, x_hi, start=False, stop=last)

            def mlp(b, fill, base, turn=None):
                def layer1(m, step, samples=slice(0, BLOCK)):
                    k = (PAIR_TILES, *range(PAIR_TILES))[step]
                    x_hi, x_lo = ((bottom_hi[:, samples], bottom_lo[:, samples]) if k == PAIR_TILES
                                  else (pairs_hi[:, k, samples], pairs_lo[:, k, samples]))
                    at = slice(m * P, (m + 1) * P)
                    return product(acc[:, (fill + m) % 2, samples], w1_hi[:, k, at], w1_lo[:, k, at], x_hi, x_lo,
                                   step == 0, step == K1 - 1 and samples.stop == BLOCK)

                ahead = 0 if turn else 2
                pe.wait_ge(bottom_split, b + 1)
                for m in range(ahead):
                    pe.wait_ge(acc_out, base + max(fill + m - 1, 0))
                    layer1(m, 0)
                if ahead:
                    pe.wait_ge(pairs_split, b * BLOCK_TILES + BLOCK_TILES - 1 + PRIME_PAIRS)
                    for m in range(ahead):
                        for step in range(1, K1):
                            layer1(m, step, slice(0, BLOCK - P))
                    pe.wait_ge(pairs_split, b * BLOCK_TILES + BLOCK_TILES + PRIME_PAIRS)
                    for m in range(ahead):
                        for step in range(1, K1):
                            last = layer1(m, step, slice(BLOCK - P, BLOCK))
                        last.then_inc(accumulated, 1)
                for m in range(ahead, M1):
                    pe.wait_ge(acc_out, base + max(fill + m - 1, 0))
                    for step in range(K1):
                        if m == 0 and step == 1:
                            pe.wait_ge(pairs_split, b * BLOCK_TILES + BLOCK_TILES + PRIME_PAIRS)
                        last = layer1(m, step)
                        if turn and (m, step) in TURN_STEPS:
                            turn(TURN_STEPS.index((m, step)))
                    last.then_inc(accumulated, 1)
                fill += M1

                pe.wait_ge(acc_out, base + fill)
                at = [slice(m * P, (m + 1) * P) for m in range(M2)]
                for k, m in [(k, m) for ks in (range(M1 - 1), (M1 - 1,)) for m in range(M2) for k in ks]:
                    if turn and (k, m) == (M1 - 1, 0):
                        for g in range(len(TURN_STEPS), GROUPS):
                            turn(g)
                    if m == 0:
                        pe.wait_ge(h1_split, b * M1 + k + 1 + PRIME_H1)
                    last = product(acc[:, (fill + m) % 2, :], w2_hi[:, k, at[m]], w2_lo[:, k, at[m]],
                                   h1_hi[:, k, :], h1_lo[:, k, :], k == 0, k == M1 - 1)
                    if k == M1 - 1:
                        last.then_inc(accumulated, 1)
                fill += M2

            def output_layer(fill, base):
                pe.wait_ge(acc_out, base + fill)
                for k in range(M2):
                    last = pe.matmul(acc[0:1, fill % 2, :], w3_sb[:, k:k + 1], h2[:, k, :],
                                     start=(k == 0), stop=(k == M2 - 1))
                last.then_inc(accumulated, 1)

            def first_gram(b, after_group1=None):
                def between(g):
                    transpose_group(b, 2, g)
                    if g == 1 and after_group1:
                        after_group1()

                pe.wait_ge(slot0_ready, b + 1)
                gram_tile(b, 0, between)

            def block_steps(b, more):
                gram_tile(b, 1, lambda g: transpose_group(b, 3, g))
                gram_tile(b, 2)
                gram_tile(b, 3)
                if more:
                    onehot_lookups(b + 1)
                    mlp(b, NH, fills_before(b), lambda g: transpose_group(b, BLOCK_TILES + 1, g))
                    first_gram(b + 1, lambda: output_layer(NH + MLP_FILLS - 1, fills_before(b)))
                else:
                    mlp(b, 0, fills_before(b))
                    output_layer(MLP_FILLS - 1, fills_before(b))

            pe.wait_ge(identity_ready, 1)
            onehot_lookups(0)
            pe.wait_ge(acc_out, NH + EXTRA)
            first_gram(0)
            pe.wait_ge(cleared, 1)
            pe.wait_ge(weights_split, 2)
            with pe.Fori(0, BLOCKS - 1) as b:
                block_steps(b, True)
            block_steps(BLOCKS - 1, False)

        def regroup(copy, q, quadrants):
            for s in quadrants:
                def of(n, c, columns):
                    return gram[QUADRANT * s:QUADRANT * s + n, q % 2, :, c - 1:c - 1 + columns].rearrange(
                        "f t k -> f k t")

                def to(t, start, n, columns):
                    return t[start:start + n, q % 2, 0:columns, :].rearrange("f k (t s) -> f s k t", s=4)[:, s]

                copy(to(aside, 0, ASIDE, ASIDE), of(ASIDE, 1, ASIDE))
                for j in range(4):
                    last = copy(to(pairs, QUADRANT * j, COLUMN_ROWS[j], PAIR_TILES),
                                of(COLUMN_ROWS[j], COLUMNS_FROM[j], PAIR_TILES))
            return last

        @block.scalar
        def _(act):
            act.sem_inc(turned_out, PRIME_TURNED)
            act.sem_inc(act_regrouped, PRIME_REGROUPED)
            act.sem_inc(out_landed, PRIME_OUT)

            def turned_group(b, q, g):
                if g == 0:
                    act.wait_ge(grammed, b * BLOCK_TILES + q + 1 - BLOCK_TILES + PRIME_GRAMMED)
                n = q * GROUPS + g
                act.wait_ge(transposed, b * BLOCK_GROUPS + n + 1 + PRIME_TRANSPOSED)
                first, size = group_of(b, q, g)
                nc.scalar.copy(
                    features[:, q % BLOCK_TILES, :, 1 + first:1 + first + size].rearrange("d b f -> d f b"),
                    turned[:, n % 2, 0:size, :]).then_inc(turned_out, 1)

            def turned_tile(b, q):
                for g in range(GROUPS):
                    turned_group(b, q, g)

            def regroup_tile(b, q, quadrants):
                act.wait_ge(grammed, b * BLOCK_TILES + q + 1 + PRIME_GRAMMED)
                act.wait_ge(pairs_split, b * BLOCK_TILES + q - 1 + PRIME_PAIRS)
                regroup(nc.scalar.copy, q, range(quadrants)).then_inc(act_regrouped, 1)

            def table_high_part(r, i):
                act.wait_ge(raw_landed[i % 2], landed(r, i))
                if i >= TABLE_RING:
                    act.wait_ge(accumulated, fills_before_round(r) + i + 1 - TABLE_RING)
                nc.scalar.copy(table_hi[0:ROW_PARTS, i % TABLE_RING], table_raw[0:ROW_PARTS, i % 2]).then_inc(
                    table_high, 1)

            def act_chunk(r, i):
                act.wait_ge(wanted_landed[i % 2], landed(r, i))
                samples = samples_of(r, i)
                at_least(act, act_chunk_ready, tables_before(r) + i)
                nc.scalar.activation(distance[0:ROW_PARTS, samples], wanted[0:ROW_PARTS, i % 2, samples], ACT.Abs,
                                     bias=row_number[0:ROW_PARTS, CHUNKS:CHUNKS + 1]).then_inc(distance_ready, 1)
                act.wait_ge(distance_ready, tables_before(r) + i + 1)
                if i >= 1:
                    act.wait_ge(onehot_used, (tables_before(r) + i - 1) * (CHUNKS - 1) + ACT_CHUNK + 1)
                nc.scalar.activation(onehot[0:ROW_PARTS, ACT_CHUNK, samples], distance[0:ROW_PARTS, samples], ACT.Relu,
                                     scale=-1.0, bias=row_number[0:ROW_PARTS, CHUNKS + 1:CHUNKS + 2]).then_inc(
                                         act_chunk_ready, 1)

            def onehot_out(r, after_first=None):
                for i in range(tables_of(r)):
                    if isinstance(r, int):
                        if i in FIRST_TURNS:
                            turned_group(0, *FIRST_TURNS[i])
                    elif i in TURNS:
                        turned_group(r - 1, *TURNS[i])
                    if i + 1 < tables_of(r):
                        act_chunk(r, i + 1)
                    act.wait_ge(accumulated, fills_before_round(r) + i + 1)
                    slot = 1 + (NG + i if i < NH else NG - EXTRA + i - NH)
                    samples = samples_of(r, i)
                    nc.scalar.copy(features[:, 0:samples.stop // P, :, slot].rearrange("d q b -> d (q b)"),
                                   acc[:, i % 2, samples]).then_inc(acc_out, 1)
                    if i + TABLES_AHEAD < tables_of(r):
                        table_high_part(r, i + TABLES_AHEAD)
                    if i == 0 and after_first:
                        after_first()
                    if isinstance(r, int) and i == tables_of(r) - TABLES_AHEAD:
                        act.wait_ge(w1_landed, 16)
                        nc.scalar.copy(w1_hi[:], w1_raw).then_inc(weights_high, 1)
                    if isinstance(r, int) and i == tables_of(r) - TABLES_AHEAD + 1:
                        act.wait_ge(w2_landed, 16)
                        nc.scalar.copy(w2_hi[:], w2_raw).then_inc(weights_high, 1)

            def mlp_out(b, fill, base, turned_of=None):
                for m in range(M1):
                    if turned_of:
                        for g, (at, _) in enumerate(TURN_STEPS):
                            if at == m:
                                turned_of(g)
                    act.wait_ge(accumulated, base + fill + 1)
                    act.wait_ge(h1_split, b * M1 + m - 1 + PRIME_H1)
                    nc.scalar.activation(h1[:, m % 2, :], acc[:, fill % 2, :], ACT.Relu,
                                         bias=b1_sb[:, m:m + 1]).then_inc(acc_out, 1)
                    fill += 1
                if turned_of:
                    for g in range(len(TURN_STEPS), GROUPS):
                        turned_of(g)
                for m in range(M2):
                    act.wait_ge(accumulated, base + fill + 1)
                    nc.scalar.activation(h2[:, m, :], acc[:, fill % 2, :], ACT.Relu,
                                         bias=b2_sb[:, m:m + 1]).then_inc(acc_out, 1)
                    fill += 1

            def output(b, fill, base):
                act.wait_ge(accumulated, base + fill + 1)
                act.wait_ge(out_landed, 16 * b + PRIME_OUT)
                nc.scalar.copy(y_sb[:], acc[0:1, fill % 2, :]).then_inc(acc_out, 1)
                gated(act, "act", acc_out, base + fill + 1)
                act.dma_start(out[:, bass.ds(b * BLOCK, BLOCK)], y_sb[:]).then_inc(out_landed, 16)

            def block_steps(b, more):
                for q in range(BLOCK_TILES - 1):
                    regroup_tile(b, q, ACT_QUADRANTS[q])
                    if q == 0:
                        turned_tile(b, 3)
                    if more:
                        for i in HIGH_PARTS[q]:
                            table_high_part(b + 1, i)
                        if q == 1:
                            act_chunk(b + 1, 0)
                if more:
                    onehot_out(b + 1, lambda: regroup_tile(b, 3, ACT_QUADRANTS[3]))
                    mlp_out(b, NH, fills_before(b), lambda g: turned_group(b, BLOCK_TILES + 1, g))
                    for g in range(GROUPS):
                        turned_group(b + 1, 2, g)
                        if g == 1:
                            output(b, NH + MLP_FILLS - 1, fills_before(b))
                else:
                    regroup_tile(b, 3, LAST_ACT_QUADRANTS)
                    mlp_out(b, 0, fills_before(b))
                    output(b, MLP_FILLS - 1, fills_before(b))

            act.dma_start(table_raw[0:ROW_PARTS, 0], onehot_tables[0].rearrange("(p c) d -> p c d", c=CHUNKS)
                          ).then_inc(raw_landed[0], 16)
            table_high_part(0, 0)
            act.wait_ge(row_number_landed, 16)
            act_chunk(0, 0)
            for i in range(1, TABLES_AHEAD):
                table_high_part(0, i)
            onehot_out(0)
            turned_tile(0, 2)
            act.wait_ge(small_landed, 3 * 16)
            act.wait_ge(cleared, 1)
            act.wait_ge(weights_split, 2)
            with act.Fori(0, BLOCKS - 1) as b:
                block_steps(b, True)
            block_steps(BLOCKS - 1, False)

        @block.vector
        def _(dve):
            dve.sem_inc(dve_regrouped, PRIME_REGROUPED)
            dve.sem_inc(pairs_split, PRIME_PAIRS)
            dve.sem_inc(h1_split, PRIME_H1)

            def table_low_part(r, i):
                dve.wait_ge(table_high, tables_before(r) + i + 1)
                dve.tensor_tensor(table_lo[0:ROW_PARTS, i % TABLE_RING], table_raw[0:ROW_PARTS, i % 2],
                                  table_hi[0:ROW_PARTS, i % TABLE_RING], ALU.subtract).then_inc(table_split, 1)

            def onehot_chunk(r, i, c):
                if c == ACT_CHUNK:
                    return
                if c == 0:
                    dve.wait_ge(wanted_landed[i % 2], landed(r, i))
                if i >= 1:
                    if c < CHUNKS - 1:
                        dve.wait_ge(onehot_used, (tables_before(r) + i - 1) * (CHUNKS - 1) + c + 1)
                    else:
                        dve.wait_ge(accumulated, fills_before_round(r) + i)
                samples = samples_of(r, i)
                dve.tensor_scalar(onehot[0:ROW_PARTS, c, samples], wanted[0:ROW_PARTS, i % 2, samples],
                                  row_number[0:ROW_PARTS, c:c + 1], None, ALU.is_equal).then_inc(onehot_ready, 1)

            def onehots(r, i, ahead):
                for c in range(CHUNKS):
                    onehot_chunk(r, i, c)
                if i + ahead < tables_of(r):
                    table_low_part(r, i + ahead)

            def fill_slot0(b):
                dve.wait_ge(bottom_landed, 16 * (b + 1))
                dve.tensor_copy(features[:, :, :, 0].rearrange("d q b -> d (q b)"), bottom[:]).then_inc(slot0_ready, 1)

            def split_bottom(b):
                dve.tensor_copy(bottom_hi[:], bottom[:]).then_inc(bottom_high, 1)
                dve.wait_ge(bottom_high, b + 1)
                dve.tensor_tensor(bottom_lo[:], bottom[:], bottom_hi[:], ALU.subtract).then_inc(bottom_split, 1)

            def regroup_tile(b, q, quadrants):
                dve.wait_ge(grammed, b * BLOCK_TILES + q + 1 + PRIME_GRAMMED)
                dve.wait_ge(pairs_split, b * BLOCK_TILES + q - 1 + PRIME_PAIRS)
                regroup(dve.tensor_copy, q, range(quadrants, 4)).then_inc(dve_regrouped, 1)

            def split_tile(b, q):
                dve.wait_ge(act_regrouped, b * BLOCK_TILES + q + 1 + PRIME_REGROUPED)
                dve.wait_ge(dve_regrouped, b * BLOCK_TILES + q + 1 + PRIME_REGROUPED)
                dve.wait_ge(aside_landed[q % 2], 16 * len(ASIDE_MOVES) * (2 * b + q // 2 + 1))
                at = slice(q * P, (q + 1) * P)
                dve.tensor_copy(pairs_hi[:, :, at], pairs[:, q % 2]).then_inc(pairs_high, 1)
                dve.wait_ge(pairs_high, b * BLOCK_TILES + q + 1)
                dve.tensor_tensor(pairs_lo[:, :, at], pairs[:, q % 2], pairs_hi[:, :, at],
                                  ALU.subtract).then_inc(pairs_split, 1)

            def split_h1(b, base):
                for m in range(M1):
                    dve.wait_ge(acc_out, base + m + 1)
                    dve.tensor_copy(h1_hi[:, m, :], h1[:, m % 2, :]).then_inc(h1_high, 1)
                    dve.wait_ge(h1_high, b * M1 + m + 1)
                    dve.tensor_tensor(h1_lo[:, m, :], h1[:, m % 2, :], h1_hi[:, m, :],
                                      ALU.subtract).then_inc(h1_split, 1)

            def block_steps(b, more):
                for q in range(BLOCK_TILES - 1):
                    regroup_tile(b, q, ACT_QUADRANTS[q])
                    if more:
                        for c in range(3 * q, min(3 * q + 3, CHUNKS)):
                            onehot_chunk(b + 1, 0, c)
                    if q:
                        split_tile(b, q - 1)
                    if more and q in LOW_PARTS:
                        for i in LOW_PARTS[q]:
                            table_low_part(b + 1, i)
                if more:
                    for i in range(1, NH):
                        onehots(b + 1, i, 1)
                        if i == 2:
                            regroup_tile(b, 3, ACT_QUADRANTS[3])
                        if i in SPLIT_AFTER:
                            split_tile(b, SPLIT_AFTER[i])
                    split_h1(b, fills_before(b) + NH)
                    fill_slot0(b + 1)
                    split_bottom(b + 1)
                else:
                    regroup_tile(b, 3, LAST_ACT_QUADRANTS)
                    split_tile(b, 2)
                    split_tile(b, 3)
                    split_h1(b, fills_before(b))

            LOW_PARTS = {1: (0, 1)}
            SPLIT_AFTER = {NH - 2: 2, NH - 1: 3}
            dve.memset(pairs[:], 0.0).then_inc(cleared, 1)
            dve.wait_ge(row_number_landed, 16)
            for c in range(CHUNKS):
                onehot_chunk(0, 0, c)
                if c == 1:
                    table_low_part(0, 0)
            for i in range(1, TABLES_AHEAD):
                table_low_part(0, i)
                if i == 1:
                    for c in range(CHUNKS):
                        onehot_chunk(0, 1, c)
            table_low_part(0, TABLES_AHEAD)
            for i in range(2, NH + EXTRA):
                onehots(0, i, 2)
            fill_slot0(0)
            split_bottom(0)
            dve.wait_ge(weights_high, 2)
            dve.tensor_tensor(w1_lo[:], w1_raw, w1_hi[:], ALU.subtract).then_inc(weights_split, 1)
            dve.tensor_tensor(w2_lo[:], w2_raw, w2_hi[:], ALU.subtract).then_inc(weights_split, 1)
            dve.wait_ge(weights_split, 2)
            dve.wait_ge(cleared, 1)
            with dve.Fori(0, BLOCKS - 1) as b:
                block_steps(b, True)
            block_steps(BLOCKS - 1, False)


def layer1_rows():
    import numpy as np

    feature = [0] + [1 + t for t in SLOT_TABLES]
    number = {}
    for f in range(SLOTS):
        for g in range(f + 1, SLOTS):
            number[f, g] = number[g, f] = len(number) // 2

    at = np.full((P, PAIR_TILES), -1)
    for k in range(PAIR_TILES):
        for j in range(4):
            g = COLUMNS_FROM[j] + k
            for f in range(g):
                at[QUADRANT * j + f, k] = number[feature[f], feature[g]]
        row = FREE_ROW
        for c, columns, n in ASIDE_MOVES:
            if k < columns:
                for f in range(c + k):
                    at[row + f, k] = number[feature[f], feature[c + k]]
            row += n
    return at, len(number) // 2


def kernel(**inputs):
    import numpy as np
    import concourse.bacc as bacc
    from concourse.bass_utils import run_bass_kernel_spmd

    a = {name: np.asarray(v) for name, v in inputs.items()}
    at, pairs = layer1_rows()
    w1 = np.zeros((P, K1, HIDDEN1), np.float32)
    w1[:, :PAIR_TILES][at >= 0] = a["W_top1"][at[at >= 0]]
    w1[:, PAIR_TILES] = a["W_top1"][pairs:]
    row_numbers = np.arange(P * CHUNKS, dtype=np.float32).reshape(P, CHUNKS)
    row_numbers = np.concatenate([row_numbers, -row_numbers[:, ACT_CHUNK:ACT_CHUNK + 1], np.ones((P, 1), np.float32)], axis=1)
    arrays = {
        "in_xT": a["r_bottom_output"].T,
        "in_ids": a["ids"][:, GATHERED].reshape(BLOCKS, 2, 2, P, NG).transpose(0, 1, 3, 2, 4).reshape(BLOCKS, 2, P, 2 * NG),
        "in_onehot_ids": a["ids"][:, FIRST_ONEHOT].T,
        "in_row_numbers": row_numbers,
        "in_w1": w1,
        "in_b1": a["b_top1"].reshape(M1, P).T,
        "in_w2": a["W_top2"].reshape(M1, P, HIDDEN2).transpose(1, 0, 2),
        "in_b2": a["b_top2"].reshape(M2, P).T,
        "in_w3": a["W_top3"].reshape(M2, P).T,
    }
    for f in range(TABLES):
        arrays[f"in_tbl_{f}"] = a[f"tbl_{f}"]
    arrays = {name: np.ascontiguousarray(x) for name, x in arrays.items()}

    nc = bacc.Bacc("TRN2", target_bir_lowering=False, num_devices=1)
    ap = {name: nc.dram_tensor(name, x.shape, mybir.dt.from_np(x.dtype), kind="ExternalInput").ap()
          for name, x in arrays.items()}
    out = nc.dram_tensor("out", (BATCH, 1), F32, kind="ExternalOutput").ap()
    dlrm_tower(nc, ap["in_xT"], ap["in_ids"], ap["in_onehot_ids"], ap["in_row_numbers"],
               [ap[f"in_tbl_{f}"] for f in GATHERED], [ap[f"in_tbl_{f}"] for f in FIRST_ONEHOT],
               ap["in_w1"], ap["in_b1"], ap["in_w2"], ap["in_b2"], ap["in_w3"],
               out.rearrange("n o -> o n"))
    r = run_bass_kernel_spmd(nc, [arrays], core_ids=[0])
    return r.results[0]["out"]
```
